# Optimizing a Trainium2 kernel written in Bass

```python
import numpy as np
import jax
import jax.numpy as jnp

def _softmax(x, axis=-1):
    return jax.nn.softmax(x, axis=axis)

def _gelu(x):
    return jax.nn.gelu(x, approximate=True)

def _silu(x):
    return jax.nn.silu(x)

def _sigmoid(x):
    return jax.nn.sigmoid(x)

def _layernorm(x, axis=-1, eps=1e-05):
    m = jnp.mean(x, axis=axis, keepdims=True)
    v = jnp.var(x, axis=axis, keepdims=True)
    return (x - m) / jnp.sqrt(v + eps)

def _scatter_add(tgt, idx, src, axis=0):
    return tgt.at[idx].add(src)

def _segment_sum(src, seg, n):
    return jax.ops.segment_sum(src, seg, n)
kernel_name = 'mk_adaln_d1_jaxref_r8_1a2652'

def setup_inputs(seed: int=0):
    np.random.seed(seed)
    _w = jnp.asarray

    def _L0_attn_setup():
        import math
        import jax, jax.numpy as jnp
        import numpy as np
        B, T, E, H = (1, 256, 256, 16)
        D = E // H // 2
        DEPTH = 12
        LAMBDA_INIT = 0.8 - 0.6 * math.exp(-0.3 * DEPTH)
        EPS = 1e-05
        NEG = -1e+30

        def rotary_cos_sin(seqlen, dim):
            inv_freq = 1.0 / 10000.0 ** (jnp.arange(0, dim, 2, dtype=jnp.float32) / dim)
            t = jnp.arange(seqlen, dtype=jnp.float32)
            freqs = jnp.outer(t, inv_freq)
            return (jnp.cos(freqs), jnp.sin(freqs))

        def apply_rotary_interleaved(x, cos, sin):
            x1 = x[..., 0::2]
            x2 = x[..., 1::2]
            c = cos[None, :, None, :]
            s = sin[None, :, None, :]
            o1 = x1 * c - x2 * s
            o2 = x1 * s + x2 * c
            return jnp.stack([o1, o2], axis=-1).reshape(x.shape)

        def causal_attn_pair(q, k, v1, v2, mask, scale):
            s = jnp.einsum('bthd,bshd->bhts', q, k) * scale
            s = jnp.where(mask, s, NEG)
            a = jax.nn.softmax(s, axis=-1)
            o1 = jnp.einsum('bhts,bshd->bthd', a, v1)
            o2 = jnp.einsum('bhts,bshd->bthd', a, v2)
            return jnp.concatenate([o1, o2], axis=-1)
        key = jax.random.key(seed)
        ks = jax.random.split(key, 10)
        return {'query': jax.random.normal(ks[0], (B, T, E), dtype=jnp.float32), 'Wq': jax.random.normal(ks[1], (E, E), dtype=jnp.float32) * 0.02, 'Wk': jax.random.normal(ks[2], (E, E), dtype=jnp.float32) * 0.02, 'Wv': jax.random.normal(ks[3], (E, E), dtype=jnp.float32) * 0.02, 'Wout': jax.random.normal(ks[4], (E, E), dtype=jnp.float32) * 0.02, 'lambda_q1': jax.random.normal(ks[5], (D,), dtype=jnp.float32) * 0.1, 'lambda_k1': jax.random.normal(ks[6], (D,), dtype=jnp.float32) * 0.1, 'lambda_q2': jax.random.normal(ks[7], (D,), dtype=jnp.float32) * 0.1, 'lambda_k2': jax.random.normal(ks[8], (D,), dtype=jnp.float32) * 0.1, 'rms_weight': jnp.ones((2 * D,), dtype=jnp.float32)}
    _L0_attn_in = _L0_attn_setup()

    def _L0_ffn_setup():
        import jax, jax.numpy as jnp
        import numpy as np
        B, S, H = (2, 128, 256)
        E, K, F = (8, 2, 176)
        N_SHARED = 2
        FS = F * N_SHARED
        ROUTED_SCALE = 1.0

        def _swiglu_mlp(x, wg, wu, wd):
            return jax.nn.silu(x @ wg.T) * (x @ wu.T) @ wd.T
        key = jax.random.key(seed)
        ks = jax.random.split(key, 8)

        def w(k, shape, fan_in):
            return jax.random.normal(k, shape, jnp.float32) * (1.0 / np.sqrt(fan_in))
        return {'hidden_states': jax.random.normal(ks[0], (B, S, H), jnp.float32), 'gate_weight': w(ks[1], (E, H), H), 'w_gate': w(ks[2], (E, F, H), H), 'w_up': w(ks[3], (E, F, H), H), 'w_down': w(ks[4], (E, H, F), F), 'sw_gate': w(ks[5], (FS, H), H), 'sw_up': w(ks[6], (FS, H), H), 'sw_down': w(ks[7], (H, FS), FS)}
    _L0_ffn_in = _L0_ffn_setup()
    _L0_c = _w((lambda *s: np.random.randn(*s).astype(np.float32) * 0.05)(2, 256))
    _L0_wmod = _w((lambda *s: np.random.randn(*s).astype(np.float32) * 0.05)(256, 6 * 256) * 256 ** (-0.5))
    _d = {'L0_attn_query': _L0_attn_in['query'], 'L0_attn_Wq': _L0_attn_in['Wq'], 'L0_attn_Wk': _L0_attn_in['Wk'], 'L0_attn_Wv': _L0_attn_in['Wv'], 'L0_attn_Wout': _L0_attn_in['Wout'], 'L0_attn_lambda_q1': _L0_attn_in['lambda_q1'], 'L0_attn_lambda_k1': _L0_attn_in['lambda_k1'], 'L0_attn_lambda_q2': _L0_attn_in['lambda_q2'], 'L0_attn_lambda_k2': _L0_attn_in['lambda_k2'], 'L0_attn_rms_weight': _L0_attn_in['rms_weight'], 'L0_ffn_gate_weight': _L0_ffn_in['gate_weight'], 'L0_ffn_w_gate': _L0_ffn_in['w_gate'], 'L0_ffn_w_up': _L0_ffn_in['w_up'], 'L0_ffn_w_down': _L0_ffn_in['w_down'], 'L0_ffn_sw_gate': _L0_ffn_in['sw_gate'], 'L0_ffn_sw_up': _L0_ffn_in['sw_up'], 'L0_ffn_sw_down': _L0_ffn_in['sw_down'], 'L0_c': _L0_c, 'L0_wmod': _L0_wmod}
    _x0 = _d['L0_attn_query']
    _d['L0_attn_query'] = jax.random.normal(jax.random.fold_in(jax.random.key(seed), 1), (2, 512, 256), dtype=_x0.dtype)
    del _x0
    return _d

def reference(L0_attn_query, L0_attn_Wq, L0_attn_Wk, L0_attn_Wv, L0_attn_Wout, L0_attn_lambda_q1, L0_attn_lambda_k1, L0_attn_lambda_q2, L0_attn_lambda_k2, L0_attn_rms_weight, L0_ffn_gate_weight, L0_ffn_w_gate, L0_ffn_w_up, L0_ffn_w_down, L0_ffn_sw_gate, L0_ffn_sw_up, L0_ffn_sw_down, L0_c, L0_wmod):

    def _L0_attn_ref(query, Wq, Wk, Wv, Wout, lambda_q1, lambda_k1, lambda_q2, lambda_k2, rms_weight):
        import math
        import jax, jax.numpy as jnp
        import numpy as np
        B, T, E, H = (1, 256, 256, 16)
        D = E // H // 2
        DEPTH = 12
        LAMBDA_INIT = 0.8 - 0.6 * math.exp(-0.3 * DEPTH)
        EPS = 1e-05
        NEG = -1e+30

        def rotary_cos_sin(seqlen, dim):
            inv_freq = 1.0 / 10000.0 ** (jnp.arange(0, dim, 2, dtype=jnp.float32) / dim)
            t = jnp.arange(seqlen, dtype=jnp.float32)
            freqs = jnp.outer(t, inv_freq)
            return (jnp.cos(freqs), jnp.sin(freqs))

        def apply_rotary_interleaved(x, cos, sin):
            x1 = x[..., 0::2]
            x2 = x[..., 1::2]
            c = cos[None, :, None, :]
            s = sin[None, :, None, :]
            o1 = x1 * c - x2 * s
            o2 = x1 * s + x2 * c
            return jnp.stack([o1, o2], axis=-1).reshape(x.shape)

        def causal_attn_pair(q, k, v1, v2, mask, scale):
            s = jnp.einsum('bthd,bshd->bhts', q, k) * scale
            s = jnp.where(mask, s, NEG)
            a = jax.nn.softmax(s, axis=-1)
            o1 = jnp.einsum('bhts,bshd->bthd', a, v1)
            o2 = jnp.einsum('bhts,bshd->bthd', a, v2)
            return jnp.concatenate([o1, o2], axis=-1)
        bsz, tgt_len, embed_dim = query.shape
        cos, sin = rotary_cos_sin(tgt_len, D)
        scale = D ** (-0.5)
        mask = jnp.tril(jnp.ones((tgt_len, tgt_len), dtype=bool))[None, None]
        q = (query @ Wq).reshape(bsz, tgt_len, 2 * H, D)
        k = (query @ Wk).reshape(bsz, tgt_len, 2 * H, D)
        v = (query @ Wv).reshape(bsz, tgt_len, H, 2, D)
        q = apply_rotary_emb = apply_rotary_interleaved(q, cos, sin)
        k = apply_rotary_interleaved(k, cos, sin)
        q = q.reshape(bsz, tgt_len, H, 2, D)
        k = k.reshape(bsz, tgt_len, H, 2, D)
        q1, q2 = (q[:, :, :, 0], q[:, :, :, 1])
        k1, k2 = (k[:, :, :, 0], k[:, :, :, 1])
        v1, v2 = (v[:, :, :, 0], v[:, :, :, 1])
        attn1 = causal_attn_pair(q1, k1, v1, v2, mask, scale)
        attn2 = causal_attn_pair(q2, k2, v1, v2, mask, scale)
        lambda_1 = jnp.exp(jnp.sum(lambda_q1 * lambda_k1))
        lambda_2 = jnp.exp(jnp.sum(lambda_q2 * lambda_k2))
        lambda_full = lambda_1 - lambda_2 + LAMBDA_INIT
        f1 = jnp.fft.rfft(attn1, axis=1)
        f2 = jnp.fft.rfft(attn2, axis=1)
        attn_freq = f1 - lambda_full * f2
        n_freq = attn_freq.shape[1]
        sigma = 0.3 / 2.0
        x = jnp.linspace(0.0, 1.0, n_freq)
        filt = jnp.exp(-0.5 * (x / sigma) ** 2)
        attn_freq = attn_freq * filt[None, :, None, None]
        attn = jnp.fft.irfft(attn_freq, n=tgt_len, axis=1)
        attn = attn * jax.lax.rsqrt(jnp.mean(attn * attn, axis=-1, keepdims=True) + EPS) * rms_weight
        attn = attn * (1.0 - LAMBDA_INIT)
        attn = attn.reshape(bsz, tgt_len, H * 2 * D)
        return attn @ Wout

    def _L0_ffn_ref(hidden_states, gate_weight, w_gate, w_up, w_down, sw_gate, sw_up, sw_down):
        import jax, jax.numpy as jnp
        import numpy as np
        B, S, H = (2, 128, 256)
        E, K, F = (8, 2, 176)
        N_SHARED = 2
        FS = F * N_SHARED
        ROUTED_SCALE = 1.0

        def _swiglu_mlp(x, wg, wu, wd):
            return jax.nn.silu(x @ wg.T) * (x @ wu.T) @ wd.T
        b, s, h = hidden_states.shape
        x = hidden_states.reshape(-1, h)
        T = x.shape[0]
        logits = x.astype(jnp.float32) @ gate_weight.astype(jnp.float32).T
        scores = jax.nn.softmax(logits, axis=-1)
        topk_w, topk_idx = jax.lax.top_k(scores, K)
        topk_w = topk_w / (jnp.sum(topk_w, axis=-1, keepdims=True) + 1e-20)
        topk_w = topk_w * ROUTED_SCALE
        cw = jnp.zeros((T, E), jnp.float32).at[jnp.arange(T)[:, None], topk_idx].add(topk_w)
        g = jax.nn.silu(jnp.einsum('th,efh->tef', x, w_gate)) * jnp.einsum('th,efh->tef', x, w_up)
        expert_out = jnp.einsum('tef,ehf->teh', g, w_down)
        y = jnp.einsum('te,teh->th', cw, expert_out).reshape(b, s, h)
        y = y + _swiglu_mlp(x, sw_gate, sw_up, sw_down).reshape(b, s, h)
        return y
    x = L0_attn_query
    mod = (_silu(L0_c) @ L0_wmod).reshape(L0_c.shape[0], 6, 1, -1)
    sa, ca, ga, sb, cb, gb = (mod[:, 0], mod[:, 1], mod[:, 2], mod[:, 3], mod[:, 4], mod[:, 5])
    ga = (2 * (ga >= 0) - 1) * jnp.maximum(jnp.abs(ga), 0.25)
    gb = (2 * (gb >= 0) - 1) * jnp.maximum(jnp.abs(gb), 0.25)
    h = _layernorm(x, axis=-1) * (1 + ca) + sa
    x = x + ga * _L0_attn_ref(h, L0_attn_Wq, L0_attn_Wk, L0_attn_Wv, L0_attn_Wout, L0_attn_lambda_q1, L0_attn_lambda_k1, L0_attn_lambda_q2, L0_attn_lambda_k2, L0_attn_rms_weight)
    h = _layernorm(x, axis=-1) * (1 + cb) + sb
    x = x + gb * _L0_ffn_ref(h, L0_ffn_gate_weight, L0_ffn_w_gate, L0_ffn_w_up, L0_ffn_w_down, L0_ffn_sw_gate, L0_ffn_sw_up, L0_ffn_sw_down)
    return x

_drawn_inputs = setup_inputs


def setup_inputs(seed=0):
    import zlib

    import numpy as np

    out = dict(_drawn_inputs(seed))
    spreads = {'L0_attn_rms_weight': (1.0, 0.6)}
    factors = {'L0_attn_Wq': 8.0,
     'L0_attn_Wk': 8.0,
     'L0_attn_Wv': 3.72,
     'L0_attn_Wout': 3.734,
     'L0_attn_lambda_q1': 200.0,
     'L0_attn_lambda_k1': 8.0,
     'L0_attn_lambda_q2': 64.0,
     'L0_attn_lambda_k2': 64.0}
    for name, (base, spread) in spreads.items():
        noise = np.random.default_rng([zlib.crc32(name.encode()), seed]).standard_normal(out[name].shape)
        drawn = base * np.exp(spread * noise) if base else spread * noise
        out[name] = jnp.asarray(drawn.astype(out[name].dtype))
    for name, factor in factors.items():
        out[name] = (out[name] * factor).astype(out[name].dtype)
    return out
```

```python
from contextlib import ExitStack
import math

import numpy as np

import concourse.bass as bass
from concourse import mybir

F32 = mybir.dt.float32
BF16 = mybir.dt.bfloat16
U32 = mybir.dt.uint32
ALU = mybir.AluOpType
ACT = mybir.ActivationFunctionType
AX = mybir.AxisListType

P = 128
B, T, E = 2, 512, 256
H = 16
D = E // H // 2
NT = T // P
KC = E // P
SUBS = 2 * H
GS = 4
NG = B * SUBS // GS
GB = NG // B
NX, F = 8, 176
FS = 2 * F
ROUTED = NX * F // P
NF = -(-(NX * F + FS) // P)
PARTS = 3
STACK = PARTS * PARTS * D
ROWS = STACK + PARTS
VW = 32
LAMBDA_INIT = 0.8 - 0.6 * math.exp(-0.3 * 12)
EPS = 1e-5
QUARTER = 1 / math.sqrt(2 * D)
ROOT_MAX = 2.0 ** 64 * (1 - 2.0 ** -24)
MEAN_MAX = 2.0 ** 124 * (1 - 2.0 ** -23)
UNITS = GS + 1
MASKS = 2 * GS + 1
ITEMS = NT * GS + 1
SENDS = (PARTS, PARTS * PARTS)
RING = 4
SEG = {0: (0, 512), 1: (512, 384), 3: (896, 128)}


class Group:

    def __init__(self, off, base=None):
        self.static = base is None
        self.slot, self.par = off % RING, off % 2
        self.n = off if base is None else base * RING + off
        self.round = off // RING if base is None else base + off // RING

    def valid(self):
        return not self.static or 0 <= self.n < NG


def wait(engine, sem, value):
    if isinstance(value, int) and value <= 0:
        return
    engine.wait_ge(sem, value)


def item_number(g, k):
    if g.static and g.n == 0:
        return k if k < 4 else k - 1
    return g.n * ITEMS - 1 + k


def transpose_number(g):
    if g.static and g.n == NG - 1:
        return NG * ITEMS - 1
    return (g.n + 1) * ITEMS - 1 + 4


def item_bank(g, k):
    if g.static and g.n == 0:
        return (k if k < 4 else k - 1) % 2
    return (g.par + k + 1) % 2


def attention_block(nc, x, c_t, w_mod, w_qkv, w_out, rms_w, lam, w_router, w_gate, w_up, w_down,
                    rope, low_pass, causal, ident, ident_b, picks, out):
    q_stack = nc.dram_tensor("q_parts", (B, KC, PARTS, D, H, T), BF16, kind="Internal").ap()
    k_stack = nc.dram_tensor("k_parts", (B, KC, PARTS, PARTS, D, H, T), BF16, kind="Internal").ap()

    with ExitStack() as ctx:
        def sb(name, shape, dt=F32):
            return ctx.enter_context(nc.sbuf_tensor(name, shape, dt))

        def sem(name):
            return ctx.enter_context(nc.semaphore(name))

        X = sb("X", [P, B * NT, E])
        XN = sb("XN", [P, B * NT, E])
        HT = sb("HT", [P, B, KC, T])
        WQKV = sb("WQKV", [P, KC, 5 * E])
        WO = sb("WO", [P, KC, E])
        WOS = sb("WOS", [P, KC, E])
        WG = sb("WG", [P, KC, NF * P])
        WU = sb("WU", [P, KC, NF * P])
        WD = sb("WD", [P, NF, E])
        LP = sb("LP", [P, NT, T])
        CAUSAL = sb("CAUSAL", [P, T])
        ID = sb("ID", [P, P])
        IDB = sb("IDB", [P, P], BF16)
        PICK = sb("PICK", [PARTS * NX, ROUTED * P], BF16)
        V = sb("V", [P, NG, NT, VW])
        U = sb("U", [P, NG, NT, 2 * 2 * D])
        VS = sb("VS", [P, 2, NT, 2, VW])
        OTS = sb("OTS", [P, 2, T])
        U1 = sb("U1", [P, 2, NT * GS, 2 * D])
        RZ = sb("RZ", [P, NT * 2, 2])
        JUNK = sb("JUNK", [P, T])
        JUNKM = sb("JUNKM", [P, 2, T], BF16)
        MX = sb("MX", [P, 2, GS * NT])
        MR = sb("MR", [P, 2, GS * NT])
        NM = sb("NM", [P, 2, PARTS, GS * NT], BF16)
        NMT = sb("NMT", [PARTS * GS * NT, 2, P], BF16)
        GAB = sb("GAB", [P, B, 2, E])
        MOD = sb("MOD", [P, 4, KC, B])
        STAT = sb("STAT", [P, B * NT, 6])
        MV = sb("MV", [P, B * NT, 2])
        RSTD = sb("RSTD", [P, B * NT])
        CT = sb("CT", [P, KC, B])
        SC = sb("SC", [P, KC, B])
        LAM = sb("LAM", [P, 4, D])
        LV = sb("LV", [P, 8])
        RMSW = sb("RMSW", [P, KC])
        WR = sb("WR", [P, KC, NX])
        IOTA = sb("IOTA", [P, NX])
        MHALF = sb("MHALF", [P, NT * H])
        MS = sb("MS", [P, B * NT, H])
        MSF = sb("MSF", [P, B * NT, H])
        CWT = sb("CWT", [PARTS * NX, B, T], BF16)
        ROUTE = sb("ROUTE", [P, 10, B * NT, NX])
        RIDX = sb("RIDX", [P, B * NT, NX], U32)
        CWP = sb("CWP", [P, B * NT, PARTS, NX], BF16)
        R1 = sb("R1", [P, 2 * UNITS * 1024])
        WMOD = R1[:, 0:3072].rearrange("p (k n) -> p k n", k=KC)
        ROPE = R1[:, 3072:5120].rearrange("p (a t) -> p a t", a=4)
        TMP = R1[:, 5120:8192].rearrange("p (r a t) -> p r a t", r=2, a=3)
        PRT = R1[:, 8192:9728].bitcast(BF16).rearrange("p (r a t) -> p r a t", r=2, a=PARTS)
        PT = R1[:, :].rearrange("p (r u n) -> p r u n", r=2, u=UNITS)
        R2 = sb("R2", [P, 8192])
        QS = R2[:, 0:4096].bitcast(BF16).rearrange("p (r s t) -> p r s t", r=RING, s=GS)
        KS = R2[:, 4096:8192].bitcast(BF16).rearrange("p (r s t) -> p r s t", r=RING, s=GS)
        FEAT = [R[:, 0:NF * T].rearrange("p (c t) -> p c t", c=NF) for R in (R1, R2)]
        AT2 = U[:, :, :, :].rearrange("p g b n -> p (g b n)")
        SQ = R1[:, 0:2048].rearrange("p (i n) -> p i n", n=E)
        CL = R1[:, 2048:4096].rearrange("p (i n) -> p i n", n=E)
        AN = XN
        AT = R2[:, 0:B * KC * T].rearrange("p (b k t) -> p b k t", b=B, k=KC)
        MT = U[:, :, :, :].rearrange("p g b n -> p (g b n)").rearrange("p (a t) -> p a t", a=4)

        PS = ctx.enter_context(nc.psum_tensor("PS", [P, 8, 512], F32))
        UNIT = [PS[:, 0:2, :].rearrange("p a n -> p (a n)"), PS[:, 2:4, :].rearrange("p a n -> p (a n)")]

        s_x = sem("x_in")
        s_cst = sem("modulation_in")
        s_wqkv = sem("qkv_weights_in")
        s_rope = sem("rope_in")
        s_att = sem("attention_tables_in")
        s_moe = sem("expert_weights_in")
        s_misc = sem("small_tables_in")
        s_tanhc = sem("c_tanh")
        s_sc = sem("c_silu")
        s_modp = sem("modulation_products")
        s_modv = sem("modulation_ready")
        s_dv = sem("vector_chain")
        s_ln = sem("normalised_tiles")
        s_tr = sem("normalised_transposed")
        s_ht = sem("h_ready")
        s_proj = sem("projection_ready")
        s_rot = sem("rotary_read_bank")
        s_rx = sem("rotated")
        s_cut = sem("scalar_parts")
        s_res = sem("pool_residues")
        s_stk = [sem("q_parts_written"), sem("k_parts_written")]
        s_vp = sem("v_product")
        s_vr = sem("v_ready")
        s_vinit = sem("value_operand_preset")
        s_ones = sem("ones_rows")
        s_ld = [sem(f"stack_in_{i}") for i in range(RING)]
        s_nmx = [sem(f"negmax_in_{i}") for i in range(RING)]
        s_it = sem("max_tile_ready")
        s_itf = sem("max_tile_used")
        s_mxc = sem("max_chain")
        s_split = sem("max_split")
        s_unit = sem("unit_ready")
        s_exp = sem("exp_done")
        s_msk = sem("masked")
        s_vs = sem("v_staged")
        s_pv = sem("pv_done")
        s_pve = sem("pv_copied")
        s_ot = sem("output_transposed")
        s_rz = sem("norm_chain")
        s_u1 = sem("normalised_heads")
        s_u = sem("head_difference")
        s_lp = sem("low_pass_ready")
        s_cl = sem("low_pass_clamped")
        s_sq = sem("squares")
        s_an = sem("rms_normed")
        s_at = sem("attention_transposed")
        s_atc = sem("attention_transposed_copied")
        s_op = sem("output_projection")
        s_x2 = sem("residual_one")
        s_pin = sem("power_input")
        s_pow = sem("power_done")
        s_seen = sem("register_wait_met")
        s_gate = sem("gate_chain")
        s_lam = sem("lambda_exp")
        s_dot = sem("lambda_dots")
        s_lg = sem("logits")
        s_le = sem("router_exp_in")
        s_lx = sem("router_exp")
        s_cwp = sem("routing_parts")
        s_cwt = sem("routing_transposed")
        s_cwc = sem("routing_copied")
        s_gu = sem("expert_products")
        s_th = sem("expert_tanh")
        s_mc = sem("expert_chain")
        s_guf = sem("expert_banks_used")
        s_dn = sem("down_ready")
        s_fy = sem("down_scaled")
        s_fo = sem("final_tiles")
        s_out = sem("out_written")

        block = ctx.enter_context(nc.Block())

        def load_group(sp, g):
            wait(sp, s_unit, (g.n - RING + 1) * UNITS)
            half = g.round % 2 if g.static else None
            qv = q_stack.rearrange("b m p d s t -> (b m) (p d) s t")
            kv = k_stack.rearrange("b m p r d s t -> (b m) (p r d) s t")
            bm = bass.ds(g.round, 1)
            for r in range(PARTS):
                sp.dma_start(QS[r * PARTS * D:(r + 1) * PARTS * D, g.slot],
                             qv[bm, :, g.slot * GS:(g.slot + 1) * GS, :].rearrange("o r s t -> (o r) s t")
                             ).then_inc(s_ld[g.slot], 16)
            sp.dma_start(KS[0:STACK, g.slot],
                         kv[bm, :, g.slot * GS:(g.slot + 1) * GS, :].rearrange("o r s t -> (o r) s t")
                         ).then_inc(s_ld[g.slot], 16)

        def send_max(sp, g):
            wait(sp, s_itf, transpose_number(g) + 1)
            n = GS * NT
            for p in range(PARTS):
                sp.dma_start(QS[STACK + p:STACK + p + 1, g.slot].rearrange("o s (b t) -> o (s b) t", t=P),
                             NMT[p * n:(p + 1) * n, g.par, :]).then_inc(s_nmx[g.slot], 16)

        @block.sync
        def _(sp):
            sp.dma_start(X[:, :, :], x.rearrange("b (n p) e -> p (b n) e", p=P)).then_inc(s_x, 16)
            sp.dma_start(WQKV[:, :, :], w_qkv).then_inc(s_wqkv, 16)
            sp.dma_start(ROPE, rope).then_inc(s_rope, 16)
            sp.dma_start(CAUSAL[:, :], causal).then_inc(s_att, 16)
            sp.dma_start(LP[:, :, :], low_pass).then_inc(s_att, 16)
            sp.dma_start(WO[:, :, :], w_out).then_inc(s_att, 16)
            sp.dma_start(WG[:, :, :], w_gate).then_inc(s_moe, 16)
            sp.dma_start(WU[:, :, :], w_up).then_inc(s_moe, 16)
            sp.dma_start(WD[:, :, :], w_down).then_inc(s_moe, 16)
            for n in range(4 * B):
                b, m, side = n // 4, n // 2 % 2, n % 2
                for p in range(PARTS):
                    if p == 0:
                        sp.wait_ge(s_cut, 2 * n + 1)
                    elif p == 1:
                        sp.wait_ge(s_cut, 2 * n + 2)
                    else:
                        sp.wait_ge(s_res, 2 * n + 2)
                    src = PRT[:, n % 2, p, :]
                    if side == 0:
                        sp.dma_start(q_stack[b, m, p].rearrange("d s t -> (d s) t"), src).then_inc(s_stk[side], 16)
                    else:
                        for r in range(PARTS):
                            sp.dma_start(k_stack[b, m, p, r].rearrange("d s t -> (d s) t"),
                                         src).then_inc(s_stk[side], 16)
            for side in range(2):
                sp.wait_ge(s_stk[side], 16 * SENDS[side] * 2 * B)
            sp.wait_ge(s_ones, 1)
            for g in range(RING):
                load_group(sp, Group(g))
            send_max(sp, Group(0))
            send_max(sp, Group(1))
            with sp.Fori(0, (NG - RING) // RING) as i:
                for u in range(RING):
                    load_group(sp, Group(u + RING, i))
                    send_max(sp, Group(u + 2, i))
            send_max(sp, Group(NG - 2))
            send_max(sp, Group(NG - 1))
            for i in range(B * NT):
                sp.wait_ge(s_fo, i + 1)
                sp.dma_start(out.rearrange("b (n p) e -> p (b n) e", p=P)[:, i, :], X[:, i, :]).then_inc(s_out, 16)
            sp.wait_ge(s_out, 16 * B * NT)

        def act_step(act, g):
            prev = Group(0)
            if g.valid():
                for u in range(UNITS):
                    act.wait_ge(s_unit, g.n * UNITS + u + 1)
                    if u == 0:
                        wait(act, s_pv, g.n - 1)
                    nc.scalar.activation(PT[:, g.par, u, :], UNIT[(g.par + u) % 2], ACT.Exp).then_inc(s_exp, 1)

        def act_copy_values(act, g):
            act.wait_ge(s_pv, g.n + 1)
            wait(act, s_ot, g.n)
            nc.scalar.copy(OTS[:, g.par, :], PS[:, 6, :]).then_inc(s_pve, 1)

        @block.scalar
        def _(act):
            act.dma_start(CT[:, :, :], c_t).then_inc(s_cst, 16)
            act.dma_start(WMOD, w_mod).then_inc(s_cst, 16)
            act.dma_start(ID[:, :], ident).then_inc(s_misc, 16)
            act.dma_start(IDB[:, :], ident_b).then_inc(s_misc, 16)
            act.dma_start(PICK[:, :], picks).then_inc(s_misc, 16)
            act.dma_start(LAM[:, :, :], lam.rearrange("p (a d) -> p a d", a=4)).then_inc(s_misc, 16)
            act.dma_start(RMSW[:, :], rms_w).then_inc(s_misc, 16)
            act.dma_start(WR[:, :, :], w_router).then_inc(s_misc, 16)
            act.wait_ge(s_cst, 32)
            nc.scalar.activation(SC[:, :, :], CT[:, :, :], ACT.Tanh, scale=0.5).then_inc(s_tanhc, 1)
            for b in range(B):
                act.wait_ge(s_modp, 2 + b)
                nc.scalar.copy(GAB[:, b].rearrange("p a n -> p (a n)"), PS[:, 5 + b, :]).then_inc(s_modv, 1)
            act.wait_ge(s_dot, 2)
            nc.scalar.activation(LV[:, 2:4], LV[:, 0:2], ACT.Exp).then_inc(s_lam, 1)
            for n in range(4 * B):
                act.wait_ge(s_rx, n + 1)
                if n >= 2:
                    act.wait_ge(s_stk[n % 2], 16 * SENDS[n % 2] * (n // 2))
                nc.scalar.copy(PRT[:, n % 2, 0, :], TMP[:, n % 2, 0, :]).then_inc(s_cut, 1)
                act.wait_ge(s_res, 2 * n + 1)
                nc.scalar.copy(PRT[:, n % 2, 1, :], TMP[:, n % 2, 1, :]).then_inc(s_cut, 1)
            for n in range(B * NT // 2):
                b = n // 2
                act.wait_ge(s_vp, n + 1)
                for j in range(2):
                    nc.scalar.copy(V[:, b * GB:(b + 1) * GB, n % 2 * 2 + j, 0:VW],
                                   PS[:, n, j * E:(j + 1) * E].rearrange("p (g w) -> p g w", w=VW)
                                   ).then_inc(s_vr, 1)
            act_step(act, Group(0))
            act_step(act, Group(1))
            act_copy_values(act, Group(0))
            with act.Fori(0, 3) as i:
                for u in range(RING):
                    act_step(act, Group(u + 2, i))
                    act_copy_values(act, Group(u + 1, i))
            for n in (14, 15):
                act_step(act, Group(n))
                act_copy_values(act, Group(n - 1))
            act_copy_values(act, Group(NG - 1))
            for n in range(B * NT):
                act.wait_ge(s_cl, n + 1)
                nc.scalar.activation(SQ[:, n, :], CL[:, n, :], ACT.Square, scale=QUARTER).then_inc(s_sq, 1)
            for n in range(B * KC):
                act.wait_ge(s_at, n + 1)
                nc.scalar.copy(AT[:, n // KC, n % KC, :], PS[:, 4 + n, :]).then_inc(s_atc, 1)
            act.wait_ge(s_le, 1)
            nc.scalar.activation(ROUTE[:, 1], ROUTE[:, 0], ACT.Exp).then_inc(s_lx, 1)
            for b in range(B):
                act.wait_ge(s_cwt, b + 1)
                nc.scalar.copy(CWT[:, b, :], PS[0:PARTS * NX, 6 + b, 0:T // 2].bitcast(BF16)).then_inc(s_cwc, 1)
            for n in range(B * NF):
                act.wait_ge(s_gu, n + 1)
                if n >= 2:
                    act.wait_ge(s_guf, n - 1)
                nc.scalar.activation(MT[:, n % 2, :], PS[:, n % 2 * 3, :], ACT.Tanh, scale=0.5).then_inc(s_th, 1)

        def inverse_root(pool, count, v):
            pool.wait_ge(s_pin, count)
            nc.gpsimd.tensor_tensor(v, v, MHALF[:, 0:v.shape[1]], ALU.pow).then_inc(s_pow, 1)

        def stage_values(pool, g):
            wait(pool, s_pv, g.n - 1)
            nc.gpsimd.tensor_copy(VS[:, g.par, :, :, 0:2 * D],
                                  V[:, bass.ds(g.n, 1), :, :].rearrange("p o b (h d) -> p (o b) h d", h=2)
                                  ).then_inc(s_vs, 1)

        def mask_group(pool, g):
            for u in range(GS):
                pool.wait_ge(s_exp, g.n * UNITS + u + 1)
                a = PT[:, g.par, u, :].rearrange("p (a n) -> p a n", a=2)[:, :, 0:P]
                pool.sem_inc(s_seen, 1)
                for v, pat in ((a, [[0, 2], [1, P]]), (PT[:, g.par, u, 896:1024], [[1, P]])):
                    nc.gpsimd.affine_select(out=v, in_=v, pattern=pat, compare_op=ALU.is_ge, fill=0.0,
                                            base=0, channel_multiplier=-1).then_inc(s_msk, 1)
            pool.wait_ge(s_exp, g.n * UNITS + UNITS)
            pool.sem_inc(s_seen, 1)
            v = PT[:, g.par, GS, :].rearrange("p (a n) -> p a n", a=GS)[:, :, 0:P]
            nc.gpsimd.affine_select(out=v, in_=v, pattern=[[0, GS], [1, P]], compare_op=ALU.is_ge, fill=0.0,
                                    base=0, channel_multiplier=-1).then_inc(s_msk, 1)

        def head_difference(pool, g):
            pool.wait_ge(s_u1, g.n + 2)
            v = U1[:, g.par].rearrange("p (b i) d -> p b i d", i=2)
            nc.gpsimd.tensor_tensor(U[:, bass.ds(g.n, 1), :, :].rearrange("p o b (h d) -> p (o b h) d", h=2),
                                    v[:, :, 0, :], v[:, :, 1, :], ALU.add).then_inc(s_u, 1)

        @block.gpsimd
        def _(pool):
            nc.gpsimd.memset(VS[:, :, :, :, :], 0.0).then_inc(s_vinit, 1)
            nc.gpsimd.memset(MHALF[:, :], -0.5).then_inc(s_u, 2)
            pool.wait_ge(s_u, 2)
            pool.wait_ge(s_vinit, 1)
            nc.gpsimd.memset(VS[:, :, :, :, 2 * D:2 * D + 1], 1.0).then_inc(s_vinit, 1)
            pool.wait_ge(s_vinit, 2)
            nc.gpsimd.memset(KS[64:96, :, :, :], 1.0).then_inc(s_ones, 1)
            pool.wait_ge(s_ones, 1)
            nc.gpsimd.iota(IOTA[:, :], pattern=[[1, NX]], base=0, channel_multiplier=0,
                           allow_small_or_imprecise_dtypes=True).then_inc(s_ones, 1)
            inverse_root(pool, 1, RSTD[:, :])
            for n in range(4 * B):
                r = n % 2
                pool.wait_ge(s_cut, 2 * n + 1)
                nc.gpsimd.tensor_tensor(TMP[:, r, 1, :], TMP[:, r, 0, :], PRT[:, r, 0, :],
                                        ALU.subtract).then_inc(s_res, 1)
                pool.wait_ge(s_cut, 2 * n + 2)
                pool.wait_ge(s_res, 2 * n + 1)
                nc.gpsimd.tensor_tensor(PRT[:, r, 2, :], TMP[:, r, 1, :], PRT[:, r, 1, :],
                                        ALU.subtract).then_inc(s_res, 1)
            pool.wait_ge(s_modv, B)
            g = GAB[:, :, :, :].rearrange("p b a n -> p (b a n)")
            up = AT2[:, 0:2 * B * E]
            low = AT2[:, 2 * B * E:4 * B * E]
            nc.gpsimd.tensor_scalar(up, g, 0.0, None, ALU.is_ge).then_inc(s_gate, 1)
            nc.gpsimd.tensor_scalar(low, g, 0.25, None, ALU.max).then_inc(s_gate, 1)
            pool.wait_ge(s_gate, 2)
            nc.gpsimd.tensor_tensor(low, low, up, ALU.mult).then_inc(s_gate, 1)
            nc.gpsimd.tensor_scalar(g, g, -0.25, None, ALU.min).then_inc(s_gate, 1)
            nc.gpsimd.tensor_scalar(up, up, -1.0, 1.0, ALU.mult, ALU.add).then_inc(s_gate, 1)
            pool.wait_ge(s_gate, 5)
            nc.gpsimd.tensor_tensor(g, g, up, ALU.mult).then_inc(s_gate, 1)
            pool.wait_ge(s_gate, 6)
            nc.gpsimd.tensor_tensor(g, g, low, ALU.add).then_inc(s_gate, 1)
            pool.wait_ge(s_gate, 7)
            pool.wait_ge(s_vr, B * NT)
            pool.wait_ge(s_vinit, 2)
            for n in range(2):
                stage_values(pool, Group(n))
                mask_group(pool, Group(n))
            with pool.Fori(0, 3) as i:
                for u in range(RING):
                    stage_values(pool, Group(u + 2, i))
                    mask_group(pool, Group(u + 2, i))
                    head_difference(pool, Group(u, i))
            for n in (14, 15):
                stage_values(pool, Group(n))
                mask_group(pool, Group(n))
                head_difference(pool, Group(n - 2))
            head_difference(pool, Group(14))
            head_difference(pool, Group(15))
            for b in range(B):
                inverse_root(pool, 2 + b, MS[:, b * NT:(b + 1) * NT, :].rearrange("p n h -> p (n h)"))
            inverse_root(pool, 4, RSTD[:, :])

        def max_tile(dve, g, k):
            n, bank = item_number(g, k), PS[:, 4 + item_bank(g, k), :]
            dve.wait_ge(s_it, n + 1)
            if k == 4:
                if g.static and g.n == 0:
                    return
                copy_max(dve, Group(0) if False else g, n, bank)
                return
            j = k if k < 4 else k - 1
            w = P * (j % NT + 1)
            dve.sem_inc(s_seen, 1)
            nc.vector.tensor_tensor_reduce(out=JUNKM[:, item_bank(g, k), 0:w], in0=bank[:, 0:w], in1=CAUSAL[:, T - w:T], scale=1.0,
                                           scalar=-3.0e38, op0=ALU.add, op1=ALU.max,
                                           accum_out=MX[:, g.par, j:j + 1]).then_inc(s_itf, 1)

        def copy_max(dve, g, n, bank):
            q = (g.par + 1) % 2
            if g.static:
                h = g.n - 3
                if h >= 0:
                    dve.wait_ge(s_nmx[h % RING], 48 * (h // RING + 1))
            else:
                dve.wait_ge(s_nmx[(g.slot + 1) % RING], g.round * 48 if g.slot < 3 else g.round * 48 + 48)
            nc.vector.tensor_copy(NMT[:, q, :], bank[0:PARTS * GS * NT, 0:P // 2].bitcast(BF16)).then_inc(s_itf, 1)

        def split_max(dve, g):
            last = item_number(g, ITEMS - 1)
            dve.wait_ge(s_itf, last + 1)
            nm = NM[:, g.par]
            nc.vector.tensor_scalar(nm[:, 0, :], MX[:, g.par], -1.0, None, ALU.mult).then_inc(s_mxc, 1)
            dve.wait_ge(s_mxc, g.n * 3 + 1)
            nc.vector.scalar_tensor_tensor(out=MR[:, g.par], in0=MX[:, g.par], scalar=-1.0, in1=nm[:, 0, :],
                                           op0=ALU.mult, op1=ALU.subtract).then_inc(s_mxc, 1)
            dve.wait_ge(s_mxc, g.n * 3 + 2)
            nc.vector.tensor_copy(nm[:, 1, :], MR[:, g.par]).then_inc(s_mxc, 1)
            dve.wait_ge(s_mxc, g.n * 3 + 3)
            nc.vector.tensor_tensor(nm[:, 2, :], MR[:, g.par], nm[:, 1, :], ALU.subtract).then_inc(s_split, 1)

        def normalise(dve, g):
            dve.wait_ge(s_ot, g.n + 1)
            o = PS[:, 7, :].rearrange("p (b w) -> p b w", w=VW)
            rz = RZ[:, :, :].rearrange("p b i -> p (b i)")
            nc.vector.reciprocal(rz, o[:, :, 2 * D]).then_inc(s_rz, 1)
            dve.wait_ge(s_rz, g.n * 2 + 1)
            nc.vector.tensor_scalar(RZ[:, :, 1], RZ[:, :, 1], LV[:, 5:6], None, ALU.mult).then_inc(s_rz, 1)
            dve.wait_ge(s_rz, g.n * 2 + 2)
            dve.wait_ge(s_u, g.n + 1)
            nc.vector.tensor_tensor(U1[:, g.par], o[:, :, 0:2 * D],
                                    rz.unsqueeze(2).to_broadcast([P, NT * GS, 2 * D]), ALU.mult).then_inc(s_u1, 1)

        def dve_step(dve, g_max, g_norm):
            for k in range(ITEMS):
                if g_max.valid():
                    max_tile(dve, g_max, k)
                if k == 8 and g_norm.valid():
                    normalise(dve, g_norm)
            if g_max.valid():
                split_max(dve, g_max)

        @block.vector
        def _(dve):
            chain, powers = [0], [0]

            def link(ins):
                chain[0] += 1
                ins.then_inc(s_dv, 1)
                dve.wait_ge(s_dv, chain[0])

            def layer_norm():
                for n in range(B * NT):
                    last = nc.vector.bn_stats(STAT[:, n, :], X[:, n, :])
                link(last)
                for n in range(B * NT):
                    last = nc.vector.bn_aggr(MV[:, n, :], STAT[:, n, :])
                link(last)
                nc.vector.tensor_scalar(RSTD[:, :], MV[:, :, 1], EPS, None, ALU.add).then_inc(s_pin, 1)
                powers[0] += 1
                dve.wait_ge(s_pow, powers[0])
                for n in range(B * NT):
                    nc.vector.tensor_scalar(XN[:, n, :], X[:, n, :], MV[:, n, 0:1], RSTD[:, n:n + 1],
                                            ALU.subtract, ALU.mult).then_inc(s_ln, 1)

            def modulate(first_count, which):
                for n in range(B * KC):
                    b, k = n // KC, n % KC
                    dve.wait_ge(s_tr, first_count + n + 1)
                    nc.vector.tensor_scalar(HT[:, b, k, :], PS[:, (4 if which else 0) + n, :],
                                            MOD[:, 2 * which + 1, k, b:b + 1], MOD[:, 2 * which, k, b:b + 1],
                                            ALU.mult, ALU.add).then_inc(s_ht, 1)

            nc.vector.memset(JUNKM[:, 0, 0:1], 0.0).then_inc(s_u1, 1)
            dve.wait_ge(s_tanhc, 1)
            link(nc.vector.scalar_tensor_tensor(out=SC[:, :, :], in0=SC[:, :, :], scalar=1.0, in1=CT[:, :, :],
                                                op0=ALU.add, op1=ALU.mult))
            nc.vector.tensor_scalar(SC[:, :, :], SC[:, :, :], 0.5, None, ALU.mult).then_inc(s_sc, 1)
            dve.wait_ge(s_misc, 96)
            for i in range(2):
                nc.vector.tensor_tensor_reduce(out=JUNK[:, 16 * i:16 * i + D], in0=LAM[:, 2 * i, :],
                                               in1=LAM[:, 2 * i + 1, :], scale=1.0, scalar=0.0, op0=ALU.mult,
                                               op1=ALU.add, accum_out=LV[:, i:i + 1]).then_inc(s_dot, 1)
            dve.wait_ge(s_x, 16)
            layer_norm()
            dve.wait_ge(s_lam, 1)
            link(nc.vector.tensor_tensor(LV[:, 4:5], LV[:, 3:4], LV[:, 2:3], ALU.subtract))
            link(nc.vector.tensor_scalar(LV[:, 5:6], LV[:, 4:5], -LAMBDA_INIT, None, ALU.add))
            dve.wait_ge(s_modp, 1)
            link(nc.vector.tensor_copy(MOD[:, :, :, :], PS[:, 7, 0:4 * KC * B].rearrange(
                "p (a k b) -> p a k b", a=4, k=KC)))
            for a in (1, 3):
                last = nc.vector.tensor_scalar(MOD[:, a], MOD[:, a], 1.0, None, ALU.add)
            link(last)
            modulate(0, 0)
            dve.wait_ge(s_att, 48)
            for k in range(KC):
                nc.vector.tensor_scalar(WOS[:, k, :], WO[:, k, :], RMSW[:, k:k + 1], 1.0 - LAMBDA_INIT,
                                        ALU.mult, ALU.mult)
            dve.wait_ge(s_rope, 16)
            for n in range(4 * B):
                r, side = n % 2, n % 2
                dve.wait_ge(s_proj, n + 1)
                if n >= 2:
                    dve.wait_ge(s_res, 2 * n - 2)
                bank = 4 + 2 * (n % 2)
                nc.vector.tensor_tensor(TMP[:, r, 0, :], PS[:, bank, :], ROPE[:, 2 * side, :], ALU.mult)
                last = nc.vector.tensor_tensor(TMP[:, r, 2, :], PS[:, bank + 1, :], ROPE[:, 2 * side + 1, :], ALU.mult)
                last.then_inc(s_rot, 1)
                dve.wait_ge(s_rot, n + 1)
                nc.vector.tensor_tensor(TMP[:, r, 0, :], TMP[:, r, 0, :], TMP[:, r, 2, :], ALU.add).then_inc(s_rx, 1)

            dve_step(dve, Group(0), Group(-1))
            dve_step(dve, Group(1), Group(-1))
            dve_step(dve, Group(2), Group(-1))
            dve_step(dve, Group(3), Group(-1))
            with dve.Fori(0, 3) as i:
                for u in range(RING):
                    dve_step(dve, Group(u + 4, i), Group(u, i))
            dve.wait_ge(s_it, NG * ITEMS)
            copy_max(dve, Group(NG), None, PS[:, 4 + (NG * ITEMS - 1) % 2, :])
            for n in range(12, 16):
                normalise(dve, Group(n))

            for n in range(B * NT):
                dve.wait_ge(s_lp, (n | 1) + 1)
                nc.vector.tensor_scalar(CL[:, n, :], PS[:, n // 2, n % 2 * E:(n % 2 + 1) * E], ROOT_MAX, -ROOT_MAX,
                                        ALU.min, ALU.max).then_inc(s_cl, 1)
            for n in range(B * NT):
                dve.wait_ge(s_sq, n + 1)
                nc.vector.tensor_reduce(MS[:, n, :], SQ[:, n, :].rearrange("p (h d) -> p h d", h=H), AX.X,
                                        ALU.add)
                if n % NT == NT - 1:
                    b = n // NT
                    ms = MS[:, b * NT:(b + 1) * NT, :]
                    link(nc.vector.memset(JUNK[:, 0:1], 0.0))
                    fin = MSF[:, b * NT:(b + 1) * NT, :]
                    link(nc.vector.tensor_scalar(fin, ms, MEAN_MAX, None, ALU.is_lt))
                    nc.vector.tensor_scalar(ms, ms, EPS, None, ALU.add).then_inc(s_pin, 1)
                    powers[0] += 1
                    dve.wait_ge(s_pow, powers[0])
                    link(nc.vector.tensor_tensor(ms, ms, fin, ALU.mult))
                    for m in range(b * NT, (b + 1) * NT):
                        nc.vector.tensor_tensor(
                            AN[:, m, :].rearrange("p (h d) -> p h d", h=H),
                            PS[:, m // 2, m % 2 * E:(m % 2 + 1) * E].rearrange("p (h d) -> p h d", h=H),
                            MS[:, m, :].unsqueeze(2).to_broadcast([P, H, 2 * D]), ALU.mult).then_inc(s_an, 1)
            dve.wait_ge(s_gate, 7)
            for n in range(B * NT):
                dve.wait_ge(s_op, (n | 1) + 1)
                link(nc.vector.tensor_tensor(SQ[:, n, :], PS[:, n // 2, n % 2 * E:(n % 2 + 1) * E],
                                             GAB[:, n // NT, 0, :], ALU.mult))
                nc.vector.tensor_tensor(X[:, n, :], X[:, n, :], SQ[:, n, :], ALU.add).then_inc(s_x2, 1)
            dve.wait_ge(s_x2, B * NT)
            dve.wait_ge(s_at, B * KC)
            layer_norm()
            modulate(B * KC, 1)

            dve.wait_ge(s_lg, 1)
            R = [ROUTE[:, i] for i in range(10)]
            lg = PS[:, 0, 0:B * NT * NX].rearrange("p (n e) -> p n e", e=NX)

            def wide(a):
                return a.to_broadcast([P, B * NT, NX])

            one = [ROUTE[:, 9, :, i:i + 1] for i in range(8)]
            link(nc.vector.tensor_reduce(ROUTE[:, 9, :, 0], lg, AX.X, ALU.max))
            nc.vector.tensor_tensor(R[0], lg, wide(one[0]), ALU.subtract).then_inc(s_le, 1)
            dve.wait_ge(s_lx, 1)
            link(nc.vector.tensor_reduce(ROUTE[:, 9, :, 1], R[1], AX.X, ALU.add))
            link(nc.vector.reciprocal(ROUTE[:, 9, :, 2], ROUTE[:, 9, :, 1]))
            link(nc.vector.tensor_tensor(R[2], R[1], wide(one[2]), ALU.mult))
            for n in range(B * NT):
                last = nc.vector.max(R[3][:, n, :], R[2][:, n, :])
            link(last)
            for n in range(B * NT):
                last = nc.vector.max_index(RIDX[:, n, :], R[3][:, n, :], R[2][:, n, :])
            link(last)
            link(nc.vector.tensor_copy(R[4], RIDX[:, :, :]))
            link(nc.vector.tensor_tensor(ROUTE[:, 9, :, 3], R[3][:, :, 0], R[3][:, :, 1], ALU.add))
            link(nc.vector.tensor_scalar(ROUTE[:, 9, :, 3], ROUTE[:, 9, :, 3], 1e-20, None, ALU.add))
            link(nc.vector.reciprocal(ROUTE[:, 9, :, 4], ROUTE[:, 9, :, 3]))
            link(nc.vector.tensor_tensor(R[5], R[3], wide(one[4]), ALU.mult))
            dve.wait_ge(s_ones, 2)
            iota = IOTA[:, :].unsqueeze(1).to_broadcast([P, B * NT, NX])
            for i in range(2):
                link(nc.vector.tensor_tensor(R[6 + i], iota, wide(R[4][:, :, i:i + 1]), ALU.is_equal))
                link(nc.vector.tensor_tensor(R[6 + i], R[6 + i], wide(R[5][:, :, i:i + 1]), ALU.mult))
            link(nc.vector.tensor_tensor(R[8], R[6], R[7], ALU.add))
            link(nc.vector.tensor_copy(CWP[:, :, 0, :], R[8]))
            link(nc.vector.tensor_tensor(R[6], R[8], CWP[:, :, 0, :], ALU.subtract))
            link(nc.vector.tensor_copy(CWP[:, :, 1, :], R[6]))
            nc.vector.tensor_tensor(CWP[:, :, 2, :], R[6], CWP[:, :, 1, :], ALU.subtract).then_inc(s_cwp, 1)

            for n in range(B * NF):
                b, c = n // NF, n % NF
                g, u, w = (PS[:, n % 2 * 3 + i, :] for i in range(3))
                dve.wait_ge(s_th, n + 1)
                a = MT[:, n % 2, :]
                t = MT[:, 2 + n % 2, :]
                link(nc.vector.scalar_tensor_tensor(out=t, in0=a, scalar=1.0, in1=g, op0=ALU.add, op1=ALU.mult))
                if c < ROUTED:
                    link(nc.vector.tensor_tensor(t, t, u, ALU.mult))
                    nc.vector.tensor_tensor(FEAT[b][:, c, :], t, w, ALU.mult).then_inc(s_guf, 1)
                else:
                    nc.vector.scalar_tensor_tensor(out=FEAT[b][:, c, :], in0=t, scalar=0.5, in1=u, op0=ALU.mult,
                                                   op1=ALU.mult).then_inc(s_guf, 1)
            for n in range(B * NT):
                dve.wait_ge(s_dn, (n | 1) + 1)
                tb = n % NT
                link(nc.vector.tensor_tensor(XN[:, n, :], PS[:, (n // NT) * 2 + tb // 2, tb % 2 * E:(tb % 2 + 1) * E],
                                             GAB[:, n // NT, 1, :], ALU.mult))
                nc.vector.tensor_tensor(X[:, n, :], X[:, n, :], XN[:, n, :], ALU.add).then_inc(s_fo, 1)

        def pe_max_tile(pe, g, k):
            n, bank = item_number(g, k), 4 + item_bank(g, k)
            if k == 4:
                if g.static and g.n == 0:
                    return
                pe.wait_ge(s_split, g.n)
                wait(pe, s_itf, n - 1)
                pe.sem_inc(s_seen, 1)
                pe_transpose_max(pe, (g.par + 1) % 2, bank)
                return
            if k == 0:
                pe.wait_ge(s_ld[g.slot], (g.round + 1) * 64)
            wait(pe, s_itf, n - 1)
            j = k if k < 4 else k - 1
            s, tb = j // NT, j % NT
            w = P * (tb + 1)
            nc.tensor.matmul(PS[:, bank, 0:w], QS[0:STACK, g.slot, s, tb * P:(tb + 1) * P],
                             KS[0:STACK, g.slot, s, 0:w], start=True, stop=True).then_inc(s_it, 1)

        def pe_transpose_max(pe, par, bank):
            nc.tensor.transpose(PS[0:PARTS * GS * NT, bank, 0:P // 2].bitcast(BF16),
                                NM[:, par].rearrange("p a n -> p (a n)"), IDB[:, :]).then_inc(s_it, 1)

        def pe_unit(pe, g, u):
            if u == 0:
                pe.wait_ge(s_nmx[g.slot], (g.round + 1) * 48)
            wait(pe, s_exp, g.n * UNITS + u - 1)
            o = UNIT[(g.par + u) % 2]
            if u < GS:
                for j, (at, w) in SEG.items():
                    last = nc.tensor.matmul(o[:, at:at + w], KS[0:ROWS, g.slot, u, j * P:(j + 1) * P],
                                            QS[0:ROWS, g.slot, u, T - w:T], start=True, stop=True)
            else:
                for s in range(GS):
                    last = nc.tensor.matmul(o[:, 2 * P * s:2 * P * (s + 1)], KS[0:ROWS, g.slot, s, 2 * P:3 * P],
                                            QS[0:ROWS, g.slot, s, 2 * P:T], start=True, stop=True)
            last.then_inc(s_unit, 1)

        def pe_values(pe, g, j):
            if j == 0:
                pe.wait_ge(s_msk, (g.n + 1) * MASKS)
                pe.wait_ge(s_vs, g.n + 1)
                wait(pe, s_pve, g.n)
            for s in range(GS):
                if j == 2:
                    src = PT[:, g.par, GS, 2 * P * s:2 * P * (s + 1)]
                else:
                    at, w = SEG[j]
                    src = PT[:, g.par, s, at:at + w]
                last = nc.tensor.matmul(PS[VW * s:VW * (s + 1), 6, j * P:T], VS[:, g.par, j, s // 2, :], src,
                                        start=(j == 0), stop=(j == 2), skip_group_check=True)
            if j == 2:
                last.then_inc(s_pv, 1)

        def pe_transpose_values(pe, g):
            pe.wait_ge(s_pve, g.n + 1)
            pe.wait_ge(s_u1, g.n + 1)
            for tb in range(NT):
                last = nc.tensor.transpose(PS[:, 7, tb * P:(tb + 1) * P], OTS[:, g.par, tb * P:(tb + 1) * P], ID[:, :])
            last.then_inc(s_ot, 1)

        def pe_step(pe, g_max, g_unit, g_val, g_tr):
            k = 0
            for u in range(UNITS):
                if g_unit.valid():
                    pe_unit(pe, g_unit, u)
                for _ in range(4 if u < 2 else 3):
                    if g_max.valid():
                        pe_max_tile(pe, g_max, k)
                    k += 1
                if g_val.valid() and u < NT:
                    pe_values(pe, g_val, (0, 1, 3, 2)[u])
                if g_tr.valid() and u == 1:
                    pe_transpose_values(pe, g_tr)

        @block.tensor
        def _(pe):
            pe.wait_ge(s_sc, 1)
            for a, which in enumerate((0, 1, 3, 4)):
                for m in range(KC):
                    at = (a * KC + m) * B
                    for k in range(KC):
                        last = nc.tensor.matmul(PS[:, 7, at:at + B], WMOD[:, k, which * E + m * P:which * E + (m + 1) * P],
                                                SC[:, k, :], start=(k == 0), stop=(k == KC - 1))
            last.then_inc(s_modp, 1)
            for b in range(B):
                for k in range(KC):
                    last = nc.tensor.matmul(PS[:, 5 + b, :], SC[:, k, b:b + 1].to_broadcast([P, P]),
                                            WMOD[:, k, :].rearrange("p (a n) -> p a n", a=2)[:, :, 2 * E:3 * E],
                                            start=(k == 0), stop=(k == KC - 1))
                last.then_inc(s_modp, 1)

            def transposes(src, bank, b, k, count):
                for tb in range(NT):
                    last = nc.tensor.transpose(PS[:, bank, tb * P:(tb + 1) * P],
                                               src[:, b * NT + tb, k * P:(k + 1) * P], ID[:, :])
                last.then_inc(count, 1)

            pe.wait_ge(s_misc, 96)
            for n in range(B * KC):
                if n % KC == 0:
                    pe.wait_ge(s_ln, (n // KC + 1) * NT)
                transposes(XN, n, n // KC, n % KC, s_tr)
            pe.wait_ge(s_wqkv, 16)
            pe.wait_ge(s_modv, B)
            for n in range(4 * B):
                b, m, side = n // 4, n // 2 % 2, n % 2
                pe.wait_ge(s_ht, (b + 1) * KC)
                if n >= 2:
                    pe.wait_ge(s_rot, n - 1)
                for i in range(2):
                    for k in range(KC):
                        at = (2 * side + i) * E + m * P
                        last = nc.tensor.matmul(PS[:, 4 + 2 * (n % 2) + i, :], WQKV[:, k, at:at + P], HT[:, b, k, :],
                                                start=(k == 0), stop=(k == KC - 1))
                last.then_inc(s_proj, 1)
            for n in range(B * NT // 2):
                for j in range(2):
                    for k in range(KC):
                        tb = n % 2 * 2 + j
                        last = nc.tensor.matmul(PS[:, n, j * E:(j + 1) * E], HT[:, n // 2, k, tb * P:(tb + 1) * P],
                                                WQKV[:, k, 4 * E:5 * E], start=(k == 0), stop=(k == KC - 1))
                last.then_inc(s_vp, 1)

            pe.wait_ge(s_rot, 4 * B)
            pe.wait_ge(s_ones, 1)
            none = Group(-1)
            for g in range(2):
                for k in range(ITEMS):
                    pe_max_tile(pe, Group(g), k)
            pe.wait_ge(s_vr, B * NT)
            pe_step(pe, Group(2), Group(0), none, none)
            pe_step(pe, Group(3), Group(1), Group(0), none)
            with pe.Fori(0, 3) as i:
                for u in range(RING):
                    pe_step(pe, Group(u + 4, i), Group(u + 2, i), Group(u + 1, i), Group(u, i))
            last = NG * ITEMS - 1
            pe.wait_ge(s_split, NG)
            pe.wait_ge(s_itf, last - 1)
            pe_transpose_max(pe, (NG - 1) % 2, 4 + last % 2)
            pe_step(pe, none, Group(14), Group(13), Group(12))
            pe_step(pe, none, Group(15), Group(14), Group(13))
            pe_step(pe, none, none, Group(15), Group(14))
            pe_transpose_values(pe, Group(15))

            pe.wait_ge(s_u, NG + 2)
            pe.wait_ge(s_exp, NG * UNITS)
            pe.wait_ge(s_att, 48)
            for n in range(B * NT):
                b, tb = n // NT, n % NT
                for k in range(NT):
                    last = nc.tensor.matmul(PS[:, n // 2, n % 2 * E:(n % 2 + 1) * E], LP[:, k, tb * P:(tb + 1) * P],
                                            U[:, b * GB:(b + 1) * GB, k, :], start=(k == 0), stop=(k == NT - 1))
                last.then_inc(s_lp, 1)
            pe.wait_ge(s_u1, NG + 1)
            pe.wait_ge(s_itf, NG * ITEMS)
            for n in range(B * KC):
                if n % KC == 0:
                    pe.wait_ge(s_an, (n // KC + 1) * NT)
                transposes(AN, 4 + n, n // KC, n % KC, s_at)
            for n in range(B * NT):
                b, tb = n // NT, n % NT
                pe.wait_ge(s_atc, (b + 1) * KC)
                for k in range(KC):
                    last = nc.tensor.matmul(PS[:, n // 2, n % 2 * E:(n % 2 + 1) * E], AT[:, b, k, tb * P:(tb + 1) * P],
                                            WOS[:, k, :], start=(k == 0), stop=(k == KC - 1))
                last.then_inc(s_op, 1)
            for n in range(B * KC):
                if n % KC == 0:
                    pe.wait_ge(s_ln, B * NT + (n // KC + 1) * NT)
                transposes(XN, 4 + n, n // KC, n % KC, s_tr)
            pe.wait_ge(s_ht, 2 * B * KC)
            for n in range(B * NT):
                b, tb = n // NT, n % NT
                for k in range(KC):
                    last = nc.tensor.matmul(PS[:, 0, n * NX:(n + 1) * NX], HT[:, b, k, tb * P:(tb + 1) * P],
                                            WR[:, k, :], start=(k == 0), stop=(k == KC - 1))
            last.then_inc(s_lg, 1)
            pe.wait_ge(s_cwp, 1)
            for b in range(B):
                for tb in range(NT):
                    last = nc.tensor.transpose(PS[0:PARTS * NX, 6 + b, tb * P // 2:(tb + 1) * P // 2].bitcast(BF16),
                                               CWP[:, b * NT + tb].rearrange("p a e -> p (a e)"), IDB[:, :])
                last.then_inc(s_cwt, 1)
            pe.wait_ge(s_cwc, B)
            pe.wait_ge(s_moe, 48)
            for n in range(B * NF):
                b, c = n // NF, n % NF
                if n >= 2:
                    pe.wait_ge(s_guf, n - 1)
                for i, W in enumerate((WG, WU)):
                    for k in range(KC):
                        last = nc.tensor.matmul(PS[:, n % 2 * 3 + i, :], W[:, k, c * P:(c + 1) * P], HT[:, b, k, :],
                                                start=(k == 0), stop=(k == KC - 1))
                if c < ROUTED:
                    last = nc.tensor.matmul(PS[:, n % 2 * 3 + 2, :], PICK[:, c * P:(c + 1) * P], CWT[:, b, :],
                                            start=True, stop=True)
                last.then_inc(s_gu, 1)
            for b in range(B):
                pe.wait_ge(s_guf, B * NF)
                for tb in range(NT):
                    for c in range(NF):
                        last = nc.tensor.matmul(PS[:, b * 2 + tb // 2, tb % 2 * E:(tb % 2 + 1) * E],
                                                FEAT[b][:, c, tb * P:(tb + 1) * P], WD[:, c, :],
                                                start=(c == 0), stop=(c == NF - 1))
                    last.then_inc(s_dn, 1)


def constants():
    pos = np.arange(T, dtype=np.float64)
    inv = 1.0 / 10000.0 ** (np.arange(0, D, 2, dtype=np.float32) / np.float32(D))
    ang = np.outer(np.arange(T, dtype=np.float32), inv.astype(np.float32)).astype(np.float64)
    d = np.arange(P) // H
    cos = np.cos(ang[:, d // 2]).T
    sin = np.sin(ang[:, d // 2]).T * np.where(d % 2, 1.0, -1.0)[:, None]
    scale = float(D) ** -0.5
    rope = np.stack([cos * scale, sin * scale, cos, sin], axis=1).astype(np.float32)
    freq = np.linspace(0.0, 1.0, T // 2 + 1)
    filt = np.exp(-0.5 * (freq / 0.15) ** 2)
    wave = np.fft.irfft(filt, n=T)
    low_pass = wave[(np.arange(T)[:, None] - np.arange(T)[None, :]) % T].astype(np.float32)
    causal = np.zeros((P, T), np.float32)
    causal[:, T - P:] = np.where(np.arange(P)[None, :] > np.arange(P)[:, None], -1e30, 0.0)
    ident = np.eye(P, dtype=np.float32)
    picks = np.zeros((PARTS, NX, ROUTED * P), np.float32)
    picks[:, np.arange(ROUTED * P) // F, np.arange(ROUTED * P)] = 0.5
    return rope, low_pass, causal, ident, picks.reshape(PARTS * NX, ROUTED * P)


def kernel(**inputs):
    import ml_dtypes
    import concourse.bacc as bacc
    from concourse.bass_utils import run_bass_kernel_spmd

    a = {k.replace("L0_", ""): np.asarray(v) for k, v in inputs.items()}
    rope, low_pass, causal, ident, picks = constants()
    d, s = np.arange(D), np.arange(H)
    order = np.concatenate([(m * H + s[None, :]) * D + d[:, None] for m in range(KC)]).reshape(-1)
    twin = np.concatenate([(m * H + s[None, :]) * D + (d ^ 1)[:, None] for m in range(KC)]).reshape(-1)
    wq, wk = a["attn_Wq"], a["attn_Wk"]

    def experts(w, sw):
        w = np.concatenate([np.transpose(w, (2, 0, 1)).reshape(E, NX * F), sw.T], axis=1)
        return np.pad(w, ((0, 0), (0, NF * P - w.shape[1])))

    down = np.concatenate([np.transpose(a["ffn_w_down"], (0, 2, 1)).reshape(NX * F, E), a["ffn_sw_down"].T])
    lam = np.concatenate([a["attn_lambda_" + k] for k in ("q1", "k1", "q2", "k2")])
    arrays = {
        "x": a["attn_query"], "c_t": a["c"].T, "w_mod": a["wmod"],
        "w_qkv": np.concatenate([wq[:, order], wq[:, twin], wk[:, order], wk[:, twin], a["attn_Wv"]], axis=1),
        "w_out": a["attn_Wout"], "rms_w": np.tile(a["attn_rms_weight"], H), "lam": np.tile(lam[None, :], (P, 1)),
        "w_router": a["ffn_gate_weight"].T,
        "w_gate": experts(a["ffn_w_gate"], a["ffn_sw_gate"]), "w_up": experts(a["ffn_w_up"], a["ffn_sw_up"]),
        "w_down": np.pad(down, ((0, NF * P - down.shape[0]), (0, 0))),
        "rope": rope, "low_pass": low_pass, "causal": causal, "ident": ident,
        "ident_b": ident.astype(ml_dtypes.bfloat16), "picks": picks.astype(ml_dtypes.bfloat16),
    }
    for name in ("c_t", "w_mod", "w_qkv", "w_out", "w_router", "w_gate", "w_up", "w_down", "low_pass"):
        v = arrays[name]
        arrays[name] = v.reshape(-1, P, v.shape[1]).transpose(1, 0, 2)
    arrays["rms_w"] = arrays["rms_w"].reshape(KC, P).T
    nc = bacc.Bacc("TRN2", target_bir_lowering=False, num_devices=1)
    feed, args = {}, []
    for name, v in arrays.items():
        v = np.ascontiguousarray(v)
        feed["in_" + name] = v
        args.append(nc.dram_tensor("in_" + name, v.shape, mybir.dt.from_np(v.dtype), kind="ExternalInput").ap())
    args.append(nc.dram_tensor("out", (B, T, E), F32, kind="ExternalOutput").ap())
    attention_block(nc, *args)
    r = run_bass_kernel_spmd(nc, [feed], core_ids=[0])
    return r.results[0]["out"]
```

```python
from contextlib import ExitStack
import math

import numpy as np

import concourse.bass as bass
from concourse import mybir

F32 = mybir.dt.float32
BF16 = mybir.dt.bfloat16
U32 = mybir.dt.uint32
ALU = mybir.AluOpType
ACT = mybir.ActivationFunctionType
AX = mybir.AxisListType

P = 128
B, T, E = 2, 512, 256
H = 16
D = E // H // 2
NT = T // P
KC = E // P
SUBS = 2 * H
GS = 4
NG = B * SUBS // GS
GB = NG // B
NX, F = 8, 176
FS = 2 * F
ROUTED = NX * F // P
NF = -(-(NX * F + FS) // P)
PARTS = 3
STACK = PARTS * PARTS * D
ROWS = STACK + PARTS
VW = 32
LAMBDA_INIT = 0.8 - 0.6 * math.exp(-0.3 * 12)
EPS = 1e-5
QUARTER = 1 / math.sqrt(2 * D)
ROOT_MAX = 2.0 ** 64 * (1 - 2.0 ** -24)
MEAN_MAX = 2.0 ** 124 * (1 - 2.0 ** -23)
PAIRS = GS // 2
PAIR_UNITS = 5
UNITS = PAIRS * PAIR_UNITS
MASKS = 3 * PAIRS
ITEMS = UNITS + 1
TURN = 5
SENDS = (PARTS, PARTS * PARTS)
RING = 4
MAX_BANK = 2


def unit_parts(u):
    pair, q = divmod(u, PAIR_UNITS)
    if q == PAIR_UNITS - 1:
        return [(2 * pair + i, 2, i * 2 * P) for i in range(2)]
    sub = 2 * pair + q // 2
    return [(sub, 4, 0)] if q % 2 == 0 else [(sub, 3, 0), (sub, 1, 3 * P)]


def exp_place(s, j):
    pair, i = divmod(s, 2)
    if j == 2:
        return pair * PAIR_UNITS + 4, i * 2 * P
    return pair * PAIR_UNITS + 2 * i + (j > 0), 3 * P if j == 3 else 0


VALUE_TURNS = (3, 5, 7, 9)
BLOCKS = ([(0, c) for c in range(ROUTED, NF)] + [(0, c) for c in range(ROUTED)] + [(1, c) for c in range(NF)])
AHEAD = 2


def tile_place(n):
    return (n // 2 + 2) % 4, n % 2 * E


class Group:

    def __init__(self, off, base=None):
        self.static = base is None
        self.slot, self.par = off % RING, off % 2
        self.n = off if base is None else base * RING + off
        self.round = off // RING if base is None else base + off // RING

    def valid(self):
        return not self.static or 0 <= self.n < NG


def wait(engine, sem, value):
    if isinstance(value, int) and value <= 0:
        return
    engine.wait_ge(sem, value)


def item_number(g, k):
    if g.static and g.n == 0:
        return k if k < TURN else k - 1
    return g.n * ITEMS - 1 + k


def transpose_number(g):
    if g.static and g.n == NG - 1:
        return NG * ITEMS - 1
    return (g.n + 1) * ITEMS - 1 + TURN


def item_slot(g, k):
    if g.static and g.n == 0:
        return item_number(g, k) % RING
    return (g.slot * ITEMS - 1 + k) % RING


def attention_block(nc, x, c_t, w_mod, w_qkv, w_out, rms_w, lam, w_router, w_gate, w_up, w_down,
                    rope, low_pass, causal, ident, ident_b, picks, out):
    q_stack = nc.dram_tensor("q_parts", (B, KC, PARTS, D, H, T), BF16, kind="Internal").ap()
    k_stack = nc.dram_tensor("k_parts", (B, KC, PARTS, PARTS, D, H, T), BF16, kind="Internal").ap()

    with ExitStack() as ctx:
        def sb(name, shape, dt=F32):
            return ctx.enter_context(nc.sbuf_tensor(name, shape, dt))

        def sem(name):
            return ctx.enter_context(nc.semaphore(name))

        X = sb("X", [P, B * NT, E])
        XN = sb("XN", [P, B * NT, E])
        HT = sb("HT", [P, B, KC, T])
        WQKV = sb("WQKV", [P, KC, 5 * E])
        WO = sb("WO", [P, KC, E])
        WOS = sb("WOS", [P, KC, E])
        WG = sb("WG", [P, KC, NF * P])
        WU = sb("WU", [P, KC, NF * P])
        WD = sb("WD", [P, NF, E])
        LP = sb("LP", [P, NT, T])
        CAUSAL = sb("CAUSAL", [P, T])
        ID = sb("ID", [P, P])
        IDB = sb("IDB", [P, P], BF16)
        PICK = sb("PICK", [PARTS * NX, ROUTED * P], BF16)
        V = sb("V", [P, NG, NT, VW])
        U = sb("U", [P, NG, NT, 2 * 2 * D])
        VS = sb("VS", [P, 2, NT, 2, VW])
        OTS = sb("OTS", [P, 2, T])
        U1 = sb("U1", [P, 2, NT * GS, 2 * D])
        RZ = sb("RZ", [P, NT * 2, 2])
        JUNK = sb("JUNK", [P, T])
        JUNKM = sb("JUNKM", [P, RING, T], BF16)
        MX = sb("MX", [P, 2, GS * NT])
        MR = sb("MR", [P, 2, GS * NT])
        NM = sb("NM", [P, 2, PARTS, GS * NT], BF16)
        NMT = sb("NMT", [PARTS * GS * NT, 2, P], BF16)
        GAB = sb("GAB", [P, B, 2, E])
        MOD = sb("MOD", [P, 4, KC, B])
        STAT = sb("STAT", [P, B * NT, 6])
        MV = sb("MV", [P, B * NT, 2])
        RSTD = sb("RSTD", [P, B * NT])
        CT = sb("CT", [P, KC, B])
        SC = sb("SC", [P, KC, B])
        LAM = sb("LAM", [P, 4, D])
        LV = sb("LV", [P, 8])
        RMSW = sb("RMSW", [P, KC])
        WR = sb("WR", [P, KC, NX])
        IOTA = sb("IOTA", [P, NX])
        MHALF = sb("MHALF", [P, B * NT])
        MS = sb("MS", [P, B * NT, H])
        MSF = sb("MSF", [P, B * NT, H])
        CWT = sb("CWT", [PARTS * NX, B, T], BF16)
        ROUTE = sb("ROUTE", [P, 10, B * NT, NX])
        RIDX = sb("RIDX", [P, B * NT, NX], U32)
        CWP = sb("CWP", [P, B * NT, PARTS, NX], BF16)
        R1 = sb("R1", [P, 2 * UNITS * T])
        WMOD = R1[:, 0:3072].rearrange("p (k n) -> p k n", k=KC)
        ROPE = R1[:, 3072:5120].rearrange("p (a t) -> p a t", a=4)
        TMP = R1[:, 5120:8192].rearrange("p (r a t) -> p r a t", r=2, a=3)
        PRT = R1[:, 8192:9728].bitcast(BF16).rearrange("p (r a t) -> p r a t", r=2, a=PARTS)
        PT = R1[:, :].rearrange("p (r u n) -> p r u n", r=2, u=UNITS)
        R2 = sb("R2", [P, 8192])
        QS = R2[:, 0:4096].bitcast(BF16).rearrange("p (r s t) -> p r s t", r=RING, s=GS)
        KS = R2[:, 4096:8192].bitcast(BF16).rearrange("p (r s t) -> p r s t", r=RING, s=GS)
        FEAT = [R[:, 0:NF * T].rearrange("p (c t) -> p c t", c=NF) for R in (R1, R2)]
        AT2 = U[:, :, :, :].rearrange("p g b n -> p (g b n)")
        SQ = R1[:, 0:2048].rearrange("p (i n) -> p i n", n=E)
        CL = R1[:, 2048:4096].rearrange("p (i n) -> p i n", n=E)
        AN = XN
        AT = R2[:, 0:B * KC * T].rearrange("p (b k t) -> p b k t", b=B, k=KC)
        MT = U[:, :, :, :].rearrange("p g b n -> p (g b n)").rearrange("p (a t) -> p a t", a=4)

        PS = ctx.enter_context(nc.psum_tensor("PS", [P, 8, 512], F32))

        s_x = sem("x_in")
        s_cst = sem("modulation_in")
        s_wqkv = sem("qkv_weights_in")
        s_rope = sem("rope_in")
        s_att = sem("attention_tables_in")
        s_moe = sem("expert_weights_in")
        s_misc = sem("small_tables_in")
        s_tanhc = sem("c_tanh")
        s_sc = sem("c_silu")
        s_modp = sem("modulation_products")
        s_modv = sem("modulation_ready")
        s_dv = sem("vector_chain")
        s_ln = sem("normalised_tiles")
        s_tr = sem("normalised_transposed")
        s_ht = sem("h_ready")
        s_proj = sem("projection_ready")
        s_rot = sem("rotary_read_bank")
        s_rx = sem("rotated")
        s_cut = sem("scalar_parts")
        s_res = sem("pool_residues")
        s_stk = [sem("q_parts_written"), sem("k_parts_written")]
        s_vp = sem("v_product")
        s_vr = sem("v_ready")
        s_vinit = sem("value_operand_preset")
        s_ones = sem("ones_rows")
        s_ld = [sem(f"stack_in_{i}") for i in range(RING)]
        s_nmx = [sem(f"negmax_in_{i}") for i in range(RING)]
        s_it = sem("max_tile_ready")
        s_itf = sem("max_tile_used")
        s_mxc = sem("max_chain")
        s_split = sem("max_split")
        s_unit = sem("unit_ready")
        s_exp = sem("exp_done")
        s_msk = sem("masked")
        s_vs = sem("v_staged")
        s_pv = sem("pv_done")
        s_pve = sem("pv_copied")
        s_ot = sem("output_transposed")
        s_rz = sem("norm_chain")
        s_u1 = sem("normalised_heads")
        s_u = sem("head_difference")
        s_lp = sem("low_pass_ready")
        s_cl = sem("low_pass_clamped")
        s_sq = sem("squares")
        s_an = sem("rms_normed")
        s_at = sem("attention_transposed")
        s_atc = sem("attention_transposed_copied")
        s_op = sem("output_projection")
        s_x2 = sem("residual_one")
        s_pin = sem("power_input")
        s_pow = sem("power_done")
        s_seen = sem("register_wait_met")
        s_gate = sem("gate_chain")
        s_lam = sem("lambda_exp")
        s_dot = sem("lambda_dots")
        s_lg = sem("logits")
        s_le = sem("router_exp_in")
        s_lx = sem("router_exp")
        s_cwp = sem("routing_parts")
        s_cwt = sem("routing_transposed")
        s_cwc = sem("routing_copied")
        s_gu = sem("expert_products")
        s_th = sem("expert_tanh")
        s_mc = sem("expert_chain")
        s_guf = sem("expert_banks_used")
        s_dn = sem("down_ready")
        s_fy = sem("down_scaled")
        s_fo = sem("final_tiles")
        s_out = sem("out_written")

        block = ctx.enter_context(nc.Block())

        def load_group(sp, g):
            wait(sp, s_unit, (g.n - RING + 1) * UNITS)
            half = g.round % 2 if g.static else None
            qv = q_stack.rearrange("b m p d s t -> (b m) (p d) s t")
            kv = k_stack.rearrange("b m p r d s t -> (b m) (p r d) s t")
            bm = bass.ds(g.round, 1)
            for r in range(PARTS):
                sp.dma_start(QS[r * PARTS * D:(r + 1) * PARTS * D, g.slot],
                             qv[bm, :, g.slot * GS:(g.slot + 1) * GS, :].rearrange("o r s t -> (o r) s t")
                             ).then_inc(s_ld[g.slot], 16)
            sp.dma_start(KS[0:STACK, g.slot],
                         kv[bm, :, g.slot * GS:(g.slot + 1) * GS, :].rearrange("o r s t -> (o r) s t")
                         ).then_inc(s_ld[g.slot], 16)

        def send_max(sp, g):
            wait(sp, s_itf, transpose_number(g) + 1)
            n = GS * NT
            for p in range(PARTS):
                sp.dma_start(QS[STACK + p:STACK + p + 1, g.slot].rearrange("o s (b t) -> o (s b) t", t=P),
                             NMT[p * n:(p + 1) * n, g.par, :]).then_inc(s_nmx[g.slot], 16)

        @block.sync
        def _(sp):
            sp.dma_start(X[:, :, :], x.rearrange("b (n p) e -> p (b n) e", p=P)).then_inc(s_x, 16)
            sp.dma_start(WQKV[:, :, :], w_qkv).then_inc(s_wqkv, 16)
            sp.dma_start(ROPE, rope).then_inc(s_rope, 16)
            sp.dma_start(CAUSAL[:, :], causal).then_inc(s_att, 16)
            sp.dma_start(LP[:, :, :], low_pass).then_inc(s_att, 16)
            sp.dma_start(WO[:, :, :], w_out).then_inc(s_att, 16)
            sp.dma_start(WG[:, :, :], w_gate).then_inc(s_moe, 16)
            sp.dma_start(WU[:, :, :], w_up).then_inc(s_moe, 16)
            sp.dma_start(WD[:, :, :], w_down).then_inc(s_moe, 16)
            for n in range(4 * B):
                b, m, side = n // 4, n // 2 % 2, n % 2
                for p in range(PARTS):
                    if p == 0:
                        sp.wait_ge(s_cut, 2 * n + 1)
                    elif p == 1:
                        sp.wait_ge(s_cut, 2 * n + 2)
                    else:
                        sp.wait_ge(s_res, 2 * n + 2)
                    src = PRT[:, n % 2, p, :]
                    if side == 0:
                        sp.dma_start(q_stack[b, m, p].rearrange("d s t -> (d s) t"), src).then_inc(s_stk[side], 16)
                    else:
                        for r in range(PARTS):
                            sp.dma_start(k_stack[b, m, p, r].rearrange("d s t -> (d s) t"),
                                         src).then_inc(s_stk[side], 16)
            for side in range(2):
                sp.wait_ge(s_stk[side], 16 * SENDS[side] * 2 * B)
            sp.wait_ge(s_ones, 1)
            for g in range(RING):
                load_group(sp, Group(g))
            send_max(sp, Group(0))
            send_max(sp, Group(1))
            with sp.Fori(0, (NG - RING) // RING) as i:
                for u in range(RING):
                    load_group(sp, Group(u + RING, i))
                    send_max(sp, Group(u + 2, i))
            send_max(sp, Group(NG - 2))
            send_max(sp, Group(NG - 1))
            for i in range(B * NT):
                sp.wait_ge(s_fo, i + 1)
                sp.dma_start(out.rearrange("b (n p) e -> p (b n) e", p=P)[:, i, :], X[:, i, :]).then_inc(s_out, 16)
            sp.wait_ge(s_out, 16 * B * NT)

        def act_step(act, g, g_val):
            for u in range(UNITS):
                if g.valid():
                    act.wait_ge(s_unit, g.n * UNITS + u + 1)
                    if u == 0:
                        wait(act, s_pv, g.n - 1)
                    nc.scalar.activation(PT[:, g.par, u, :], PS[:, u % 2, :], ACT.Exp).then_inc(s_exp, 1)
                if u == UNITS - 2 and g_val.valid():
                    act_copy_values(act, g_val)

        def root(act, count, v):
            act.wait_ge(s_pin, count)
            nc.scalar.activation(v, v, ACT.Sqrt).then_inc(s_pow, 1)

        def act_copy_values(act, g):
            act.wait_ge(s_pv, g.n + 1)
            wait(act, s_ot, g.n)
            nc.scalar.copy(OTS[:, g.par, :], PS[:, 6, :]).then_inc(s_pve, 1)

        @block.scalar
        def _(act):
            act.dma_start(CT[:, :, :], c_t).then_inc(s_cst, 16)
            act.dma_start(WMOD, w_mod).then_inc(s_cst, 16)
            act.dma_start(ID[:, :], ident).then_inc(s_misc, 16)
            act.dma_start(IDB[:, :], ident_b).then_inc(s_misc, 16)
            act.dma_start(PICK[:, :], picks).then_inc(s_misc, 16)
            act.dma_start(LAM[:, :, :], lam.rearrange("p (a d) -> p a d", a=4)).then_inc(s_misc, 16)
            act.dma_start(RMSW[:, :], rms_w).then_inc(s_misc, 16)
            act.dma_start(WR[:, :, :], w_router).then_inc(s_misc, 16)
            act.wait_ge(s_cst, 32)
            nc.scalar.activation(SC[:, :, :], CT[:, :, :], ACT.Tanh, scale=0.5).then_inc(s_tanhc, 1)
            for b in range(B):
                act.wait_ge(s_modp, 2 + b)
                nc.scalar.copy(GAB[:, b].rearrange("p a n -> p (a n)"), PS[:, 5 + b, :]).then_inc(s_modv, 1)
            act.wait_ge(s_dot, 2)
            nc.scalar.activation(LV[:, 2:4], LV[:, 0:2], ACT.Exp).then_inc(s_lam, 1)
            for n in range(4 * B):
                act.wait_ge(s_rx, n + 1)
                if n >= 2:
                    act.wait_ge(s_stk[n % 2], 16 * SENDS[n % 2] * (n // 2))
                nc.scalar.copy(PRT[:, n % 2, 0, :], TMP[:, n % 2, 0, :]).then_inc(s_cut, 1)
                act.wait_ge(s_res, 2 * n + 1)
                nc.scalar.copy(PRT[:, n % 2, 1, :], TMP[:, n % 2, 1, :]).then_inc(s_cut, 1)
            for n in range(B * NT // 2):
                b = n // 2
                act.wait_ge(s_vp, n + 1)
                for j in range(2):
                    nc.scalar.copy(V[:, b * GB:(b + 1) * GB, n % 2 * 2 + j, 0:VW],
                                   PS[:, n, j * E:(j + 1) * E].rearrange("p (g w) -> p g w", w=VW)
                                   ).then_inc(s_vr, 1)
            act_step(act, Group(0), Group(-1))
            act_step(act, Group(1), Group(0))
            with act.Fori(0, 3) as i:
                for u in range(RING):
                    act_step(act, Group(u + 2, i), Group(u + 1, i))
            for n in (NG - 2, NG - 1):
                act_step(act, Group(n), Group(n - 1))
            act_copy_values(act, Group(NG - 1))
            for n in range(B * NT):
                act.wait_ge(s_cl, n + 1)
                nc.scalar.activation(SQ[:, n, :], CL[:, n, :], ACT.Square, scale=QUARTER).then_inc(s_sq, 1)
                if n % NT == NT - 1:
                    b = n // NT
                    root(act, 2 + b, MS[:, b * NT:(b + 1) * NT, :])
            for n in range(B * KC):
                act.wait_ge(s_at, n + 1)
                nc.scalar.copy(AT[:, n // KC, n % KC, :], PS[:, 4 + n, :]).then_inc(s_atc, 1)
            act.wait_ge(s_le, 1)
            nc.scalar.activation(ROUTE[:, 1], ROUTE[:, 0], ACT.Exp).then_inc(s_lx, 1)
            for n in range(B * NF):
                for b in range(B if n == AHEAD else 0):
                    act.wait_ge(s_cwt, b + 1)
                    nc.scalar.copy(CWT[:, b, :], PS[0:PARTS * NX, 6 + b, 0:T // 2].bitcast(BF16)).then_inc(s_cwc, 1)
                act.wait_ge(s_gu, n + 1)
                if n >= 2:
                    act.wait_ge(s_guf, n - 1)
                nc.scalar.activation(MT[:, n % 2, :], PS[:, n % 2 * 3, :], ACT.Tanh, scale=0.5).then_inc(s_th, 1)

        def inverse_root(pool, count, v):
            pool.wait_ge(s_pin, count)
            nc.gpsimd.tensor_tensor(v, v, MHALF[:, 0:v.shape[1]], ALU.pow).then_inc(s_pow, 1)

        def stage_values(pool, g):
            wait(pool, s_pv, g.n - 1)
            nc.gpsimd.tensor_copy(VS[:, g.par, :, :, 0:2 * D],
                                  V[:, bass.ds(g.n, 1), :, :].rearrange("p o b (h d) -> p (o b) h d", h=2)
                                  ).then_inc(s_vs, 1)

        def mask_group(pool, g):
            for pair in range(PAIRS):
                u = pair * PAIR_UNITS
                pool.wait_ge(s_exp, g.n * UNITS + u + PAIR_UNITS)
                pool.sem_inc(s_seen, 1)
                four = PT[:, g.par, u:u + 4, :]
                last = PT[:, g.par, u + 4, :].rearrange("p (a n) -> p a n", a=2)
                for v, n in ((four[:, :, 0:P], 4),
                             (four.rearrange("p (a b) n -> p a b n", a=2)[:, :, 1, 3 * P:4 * P], 2),
                             (last[:, :, 0:P], 2)):
                    nc.gpsimd.affine_select(out=v, in_=v, pattern=[[0, n], [1, P]], compare_op=ALU.is_ge, fill=0.0,
                                            base=0, channel_multiplier=-1).then_inc(s_msk, 1)

        def head_difference(pool, g):
            pool.wait_ge(s_u1, g.n + 2)
            v = U1[:, g.par].rearrange("p (b i) d -> p b i d", i=2)
            nc.gpsimd.tensor_tensor(U[:, bass.ds(g.n, 1), :, :].rearrange("p o b (h d) -> p (o b h) d", h=2),
                                    v[:, :, 0, :], v[:, :, 1, :], ALU.add).then_inc(s_u, 1)

        @block.gpsimd
        def _(pool):
            nc.gpsimd.memset(VS[:, :, :, :, :], 0.0).then_inc(s_vinit, 1)
            nc.gpsimd.memset(MHALF[:, :], -0.5).then_inc(s_u, 2)
            pool.wait_ge(s_u, 2)
            pool.wait_ge(s_vinit, 1)
            nc.gpsimd.memset(VS[:, :, :, :, 2 * D:2 * D + 1], 1.0).then_inc(s_vinit, 1)
            pool.wait_ge(s_vinit, 2)
            nc.gpsimd.memset(KS[64:96, :, :, :], 1.0).then_inc(s_ones, 1)
            pool.wait_ge(s_ones, 1)
            nc.gpsimd.iota(IOTA[:, :], pattern=[[1, NX]], base=0, channel_multiplier=0,
                           allow_small_or_imprecise_dtypes=True).then_inc(s_ones, 1)
            inverse_root(pool, 1, RSTD[:, :])
            for n in range(4 * B):
                r = n % 2
                pool.wait_ge(s_cut, 2 * n + 1)
                nc.gpsimd.tensor_tensor(TMP[:, r, 1, :], TMP[:, r, 0, :], PRT[:, r, 0, :],
                                        ALU.subtract).then_inc(s_res, 1)
                pool.wait_ge(s_cut, 2 * n + 2)
                pool.wait_ge(s_res, 2 * n + 1)
                nc.gpsimd.tensor_tensor(PRT[:, r, 2, :], TMP[:, r, 1, :], PRT[:, r, 1, :],
                                        ALU.subtract).then_inc(s_res, 1)
            pool.wait_ge(s_modv, B)
            g = GAB[:, :, :, :].rearrange("p b a n -> p (b a n)")
            up = AT2[:, 0:2 * B * E]
            low = AT2[:, 2 * B * E:4 * B * E]
            nc.gpsimd.tensor_scalar(up, g, 0.0, None, ALU.is_ge).then_inc(s_gate, 1)
            nc.gpsimd.tensor_scalar(low, g, 0.25, None, ALU.max).then_inc(s_gate, 1)
            pool.wait_ge(s_gate, 2)
            nc.gpsimd.tensor_tensor(low, low, up, ALU.mult).then_inc(s_gate, 1)
            nc.gpsimd.tensor_scalar(g, g, -0.25, None, ALU.min).then_inc(s_gate, 1)
            nc.gpsimd.tensor_scalar(up, up, -1.0, 1.0, ALU.mult, ALU.add).then_inc(s_gate, 1)
            pool.wait_ge(s_gate, 5)
            nc.gpsimd.tensor_tensor(g, g, up, ALU.mult).then_inc(s_gate, 1)
            pool.wait_ge(s_gate, 6)
            nc.gpsimd.tensor_tensor(g, g, low, ALU.add).then_inc(s_gate, 1)
            pool.wait_ge(s_gate, 7)
            pool.wait_ge(s_vr, B * NT)
            pool.wait_ge(s_vinit, 2)
            for n in range(2):
                stage_values(pool, Group(n))
                mask_group(pool, Group(n))
            with pool.Fori(0, 3) as i:
                for u in range(RING):
                    stage_values(pool, Group(u + 2, i))
                    mask_group(pool, Group(u + 2, i))
                    head_difference(pool, Group(u, i))
            for n in (14, 15):
                stage_values(pool, Group(n))
                mask_group(pool, Group(n))
                head_difference(pool, Group(n - 2))
            head_difference(pool, Group(14))
            head_difference(pool, Group(15))
            inverse_root(pool, 4, RSTD[:, :])

        def max_tile(dve, g, k):
            if k == TURN and g.static and g.n == 0:
                return
            slot = item_slot(g, k)
            bank = PS[:, MAX_BANK + slot, :]
            dve.wait_ge(s_it, item_number(g, k) + 1)
            if k == TURN:
                copy_max(dve, g, bank)
                return
            dve.sem_inc(s_seen, 1)
            for s, blocks, at in unit_parts(k if k < TURN else k - 1):
                w, j = blocks * P, s * NT + blocks - 1
                last = nc.vector.tensor_tensor_reduce(out=JUNKM[:, slot, at:at + w], in0=bank[:, at:at + w],
                                                      in1=CAUSAL[:, T - w:T], scale=1.0, scalar=-3.0e38,
                                                      op0=ALU.add, op1=ALU.max, accum_out=MX[:, g.par, j:j + 1])
            last.then_inc(s_itf, 1)

        def copy_max(dve, g, bank):
            q = (g.par + 1) % 2
            if g.static:
                h = g.n - 3
                if h >= 0:
                    dve.wait_ge(s_nmx[h % RING], 48 * (h // RING + 1))
            else:
                dve.wait_ge(s_nmx[(g.slot + 1) % RING], g.round * 48 if g.slot < 3 else g.round * 48 + 48)
            nc.vector.tensor_copy(NMT[:, q, :], bank[0:PARTS * GS * NT, 0:P // 2].bitcast(BF16)).then_inc(s_itf, 1)

        def split_max(dve, g):
            last = item_number(g, ITEMS - 1)
            dve.wait_ge(s_itf, last + 1)
            nm = NM[:, g.par]
            nc.vector.tensor_scalar(nm[:, 0, :], MX[:, g.par], -1.0, None, ALU.mult).then_inc(s_mxc, 1)
            dve.wait_ge(s_mxc, g.n * 3 + 1)
            nc.vector.scalar_tensor_tensor(out=MR[:, g.par], in0=MX[:, g.par], scalar=-1.0, in1=nm[:, 0, :],
                                           op0=ALU.mult, op1=ALU.subtract).then_inc(s_mxc, 1)
            dve.wait_ge(s_mxc, g.n * 3 + 2)
            nc.vector.tensor_copy(nm[:, 1, :], MR[:, g.par]).then_inc(s_mxc, 1)
            dve.wait_ge(s_mxc, g.n * 3 + 3)
            nc.vector.tensor_tensor(nm[:, 2, :], MR[:, g.par], nm[:, 1, :], ALU.subtract).then_inc(s_split, 1)

        def normalise(dve, g):
            dve.wait_ge(s_ot, g.n + 1)
            o = PS[:, 7, :].rearrange("p (b w) -> p b w", w=VW)
            rz = RZ[:, :, :].rearrange("p b i -> p (b i)")
            nc.vector.reciprocal(rz, o[:, :, 2 * D]).then_inc(s_rz, 1)
            dve.wait_ge(s_rz, g.n * 2 + 1)
            nc.vector.tensor_scalar(RZ[:, :, 1], RZ[:, :, 1], LV[:, 5:6], None, ALU.mult).then_inc(s_rz, 1)
            dve.wait_ge(s_rz, g.n * 2 + 2)
            dve.wait_ge(s_u, g.n + 1)
            nc.vector.tensor_tensor(U1[:, g.par], o[:, :, 0:2 * D],
                                    rz.unsqueeze(2).to_broadcast([P, NT * GS, 2 * D]), ALU.mult).then_inc(s_u1, 1)

        def dve_step(dve, g_max, g_norm):
            for k in range(ITEMS):
                if g_max.valid():
                    max_tile(dve, g_max, k)
                if k == 5 and g_norm.valid():
                    normalise(dve, g_norm)
            if g_max.valid():
                split_max(dve, g_max)

        @block.vector
        def _(dve):
            chain, powers = [0], [0]

            def link(ins):
                chain[0] += 1
                ins.then_inc(s_dv, 1)
                dve.wait_ge(s_dv, chain[0])

            def layer_norm():
                for n in range(B * NT):
                    last = nc.vector.bn_stats(STAT[:, n, :], X[:, n, :])
                link(last)
                for n in range(B * NT):
                    last = nc.vector.bn_aggr(MV[:, n, :], STAT[:, n, :])
                link(last)
                nc.vector.tensor_scalar(RSTD[:, :], MV[:, :, 1], EPS, None, ALU.add).then_inc(s_pin, 1)
                powers[0] += 1
                dve.wait_ge(s_pow, powers[0])
                for n in range(B * NT):
                    nc.vector.tensor_scalar(XN[:, n, :], X[:, n, :], MV[:, n, 0:1], RSTD[:, n:n + 1],
                                            ALU.subtract, ALU.mult).then_inc(s_ln, 1)

            def modulate(first_count, which):
                for n in range(B * KC):
                    b, k = n // KC, n % KC
                    dve.wait_ge(s_tr, first_count + n + 1)
                    nc.vector.tensor_scalar(HT[:, b, k, :], PS[:, (4 if which else 0) + n, :],
                                            MOD[:, 2 * which + 1, k, b:b + 1], MOD[:, 2 * which, k, b:b + 1],
                                            ALU.mult, ALU.add).then_inc(s_ht, 1)

            nc.vector.memset(JUNKM[:, 0, 0:1], 0.0).then_inc(s_u1, 1)
            dve.wait_ge(s_tanhc, 1)
            link(nc.vector.scalar_tensor_tensor(out=SC[:, :, :], in0=SC[:, :, :], scalar=1.0, in1=CT[:, :, :],
                                                op0=ALU.add, op1=ALU.mult))
            nc.vector.tensor_scalar(SC[:, :, :], SC[:, :, :], 0.5, None, ALU.mult).then_inc(s_sc, 1)
            dve.wait_ge(s_misc, 96)
            for i in range(2):
                nc.vector.tensor_tensor_reduce(out=JUNK[:, 16 * i:16 * i + D], in0=LAM[:, 2 * i, :],
                                               in1=LAM[:, 2 * i + 1, :], scale=1.0, scalar=0.0, op0=ALU.mult,
                                               op1=ALU.add, accum_out=LV[:, i:i + 1]).then_inc(s_dot, 1)
            dve.wait_ge(s_x, 16)
            layer_norm()
            dve.wait_ge(s_lam, 1)
            link(nc.vector.tensor_tensor(LV[:, 4:5], LV[:, 3:4], LV[:, 2:3], ALU.subtract))
            link(nc.vector.tensor_scalar(LV[:, 5:6], LV[:, 4:5], -LAMBDA_INIT, None, ALU.add))
            dve.wait_ge(s_modp, 1)
            link(nc.vector.tensor_copy(MOD[:, :, :, :], PS[:, 7, 0:4 * KC * B].rearrange(
                "p (a k b) -> p a k b", a=4, k=KC)))
            for a in (1, 3):
                last = nc.vector.tensor_scalar(MOD[:, a], MOD[:, a], 1.0, None, ALU.add)
            link(last)
            modulate(0, 0)
            dve.wait_ge(s_att, 48)
            for k in range(KC):
                nc.vector.tensor_scalar(WOS[:, k, :], WO[:, k, :], RMSW[:, k:k + 1], 1.0 - LAMBDA_INIT,
                                        ALU.mult, ALU.mult)
            dve.wait_ge(s_rope, 16)
            for n in range(4 * B):
                r, side = n % 2, n % 2
                dve.wait_ge(s_proj, n + 1)
                if n >= 2:
                    dve.wait_ge(s_res, 2 * n - 2)
                bank = 4 + 2 * (n % 2)
                nc.vector.tensor_tensor(TMP[:, r, 0, :], PS[:, bank, :], ROPE[:, 2 * side, :], ALU.mult)
                last = nc.vector.tensor_tensor(TMP[:, r, 2, :], PS[:, bank + 1, :], ROPE[:, 2 * side + 1, :], ALU.mult)
                last.then_inc(s_rot, 1)
                dve.wait_ge(s_rot, n + 1)
                nc.vector.tensor_tensor(TMP[:, r, 0, :], TMP[:, r, 0, :], TMP[:, r, 2, :], ALU.add).then_inc(s_rx, 1)

            dve_step(dve, Group(0), Group(-1))
            dve_step(dve, Group(1), Group(-1))
            dve_step(dve, Group(2), Group(-1))
            dve_step(dve, Group(3), Group(-1))
            with dve.Fori(0, 3) as i:
                for u in range(RING):
                    dve_step(dve, Group(u + 4, i), Group(u, i))
            dve.wait_ge(s_it, NG * ITEMS)
            copy_max(dve, Group(NG), PS[:, MAX_BANK + (NG * ITEMS - 1) % RING, :])
            for n in range(12, 16):
                normalise(dve, Group(n))

            for n in range(B * NT):
                dve.wait_ge(s_lp, (n | 1) + 1)
                bank, at = tile_place(n)
                nc.vector.tensor_scalar(CL[:, n, :], PS[:, bank, at:at + E], ROOT_MAX, -ROOT_MAX,
                                        ALU.min, ALU.max).then_inc(s_cl, 1)
            for n in range(B * NT):
                dve.wait_ge(s_sq, n + 1)
                nc.vector.tensor_reduce(MS[:, n, :], SQ[:, n, :].rearrange("p (h d) -> p h d", h=H), AX.X,
                                        ALU.add)
                if n % NT == NT - 1:
                    b = n // NT
                    ms = MS[:, b * NT:(b + 1) * NT, :]
                    link(nc.vector.memset(JUNK[:, 0:1], 0.0))
                    fin = MSF[:, b * NT:(b + 1) * NT, :]
                    link(nc.vector.tensor_scalar(fin, ms, MEAN_MAX, None, ALU.is_lt))
                    link(nc.vector.tensor_scalar(ms, ms, EPS, None, ALU.add))
                    nc.vector.reciprocal(ms, ms).then_inc(s_pin, 1)
                    powers[0] += 1
                    dve.wait_ge(s_pow, powers[0])
                    link(nc.vector.tensor_tensor(ms, ms, fin, ALU.mult))
                    for m in range(b * NT, (b + 1) * NT):
                        bank, at = tile_place(m)
                        nc.vector.tensor_tensor(
                            AN[:, m, :].rearrange("p (h d) -> p h d", h=H),
                            PS[:, bank, at:at + E].rearrange("p (h d) -> p h d", h=H),
                            MS[:, m, :].unsqueeze(2).to_broadcast([P, H, 2 * D]), ALU.mult).then_inc(s_an, 1)
            dve.wait_ge(s_gate, 7)
            for n in range(B * NT):
                dve.wait_ge(s_op, (n | 1) + 1)
                bank, at = tile_place(n)
                link(nc.vector.tensor_tensor(SQ[:, n, :], PS[:, bank, at:at + E],
                                             GAB[:, n // NT, 0, :], ALU.mult))
                nc.vector.tensor_tensor(X[:, n, :], X[:, n, :], SQ[:, n, :], ALU.add).then_inc(s_x2, 1)
            dve.wait_ge(s_x2, B * NT)
            dve.wait_ge(s_at, B * KC)
            layer_norm()
            modulate(B * KC, 1)

            dve.wait_ge(s_lg, 1)
            R = [ROUTE[:, i] for i in range(10)]
            lg = PS[:, 6, 0:B * NT * NX].rearrange("p (n e) -> p n e", e=NX)

            def wide(a):
                return a.to_broadcast([P, B * NT, NX])

            one = [ROUTE[:, 9, :, i:i + 1] for i in range(8)]
            link(nc.vector.tensor_reduce(ROUTE[:, 9, :, 0], lg, AX.X, ALU.max))
            nc.vector.tensor_tensor(R[0], lg, wide(one[0]), ALU.subtract).then_inc(s_le, 1)
            dve.wait_ge(s_lx, 1)
            link(nc.vector.tensor_reduce(ROUTE[:, 9, :, 1], R[1], AX.X, ALU.add))
            link(nc.vector.reciprocal(ROUTE[:, 9, :, 2], ROUTE[:, 9, :, 1]))
            link(nc.vector.tensor_tensor(R[2], R[1], wide(one[2]), ALU.mult))
            for n in range(B * NT):
                last = nc.vector.max(R[3][:, n, :], R[2][:, n, :])
            link(last)
            for n in range(B * NT):
                last = nc.vector.max_index(RIDX[:, n, :], R[3][:, n, :], R[2][:, n, :])
            link(last)
            link(nc.vector.tensor_copy(R[4], RIDX[:, :, :]))
            link(nc.vector.tensor_tensor(ROUTE[:, 9, :, 3], R[3][:, :, 0], R[3][:, :, 1], ALU.add))
            link(nc.vector.tensor_scalar(ROUTE[:, 9, :, 3], ROUTE[:, 9, :, 3], 1e-20, None, ALU.add))
            link(nc.vector.reciprocal(ROUTE[:, 9, :, 4], ROUTE[:, 9, :, 3]))
            link(nc.vector.tensor_tensor(R[5], R[3], wide(one[4]), ALU.mult))
            dve.wait_ge(s_ones, 2)
            iota = IOTA[:, :].unsqueeze(1).to_broadcast([P, B * NT, NX])
            for i in range(2):
                link(nc.vector.tensor_tensor(R[6 + i], iota, wide(R[4][:, :, i:i + 1]), ALU.is_equal))
                link(nc.vector.tensor_tensor(R[6 + i], R[6 + i], wide(R[5][:, :, i:i + 1]), ALU.mult))
            link(nc.vector.tensor_tensor(R[8], R[6], R[7], ALU.add))
            link(nc.vector.tensor_copy(CWP[:, :, 0, :], R[8]))
            link(nc.vector.tensor_tensor(R[6], R[8], CWP[:, :, 0, :], ALU.subtract))
            link(nc.vector.tensor_copy(CWP[:, :, 1, :], R[6]))
            nc.vector.tensor_tensor(CWP[:, :, 2, :], R[6], CWP[:, :, 1, :], ALU.subtract).then_inc(s_cwp, 1)

            for n, (b, c) in enumerate(BLOCKS):
                g, u, w = (PS[:, n % 2 * 3 + i, :] for i in range(3))
                dve.wait_ge(s_th, n + 1)
                a = MT[:, n % 2, :]
                t = MT[:, 2 + n % 2, :]
                link(nc.vector.scalar_tensor_tensor(out=t, in0=a, scalar=1.0, in1=g, op0=ALU.add, op1=ALU.mult))
                if c < ROUTED:
                    link(nc.vector.tensor_tensor(t, t, u, ALU.mult))
                    nc.vector.tensor_tensor(FEAT[b][:, c, :], t, w, ALU.mult).then_inc(s_guf, 1)
                else:
                    nc.vector.scalar_tensor_tensor(out=FEAT[b][:, c, :], in0=t, scalar=0.5, in1=u, op0=ALU.mult,
                                                   op1=ALU.mult).then_inc(s_guf, 1)
            for n in range(B * NT):
                dve.wait_ge(s_dn, (n | 1) + 1)
                tb = n % NT
                link(nc.vector.tensor_tensor(XN[:, n, :], PS[:, (n // NT) * 2 + tb // 2, tb % 2 * E:(tb % 2 + 1) * E],
                                             GAB[:, n // NT, 1, :], ALU.mult))
                nc.vector.tensor_tensor(X[:, n, :], X[:, n, :], XN[:, n, :], ALU.add).then_inc(s_fo, 1)

        def pe_max_tile(pe, g, k):
            if k == TURN and g.static and g.n == 0:
                return
            n, bank = item_number(g, k), MAX_BANK + item_slot(g, k)
            if k == TURN:
                pe.wait_ge(s_split, g.n)
            if k == 0:
                pe.wait_ge(s_ld[g.slot], (g.round + 1) * 64)
            wait(pe, s_itf, n - RING + 1)
            if k == TURN:
                pe.sem_inc(s_seen, 1)
                pe_transpose_max(pe, (g.par + 1) % 2, bank)
                return
            for s, blocks, at in unit_parts(k if k < TURN else k - 1):
                last = nc.tensor.matmul(PS[:, bank, at:at + blocks * P],
                                        QS[0:STACK, g.slot, s, (blocks - 1) * P:blocks * P],
                                        KS[0:STACK, g.slot, s, 0:blocks * P], start=True, stop=True)
            last.then_inc(s_it, 1)

        def pe_transpose_max(pe, par, bank):
            nc.tensor.transpose(PS[0:PARTS * GS * NT, bank, 0:P // 2].bitcast(BF16),
                                NM[:, par].rearrange("p a n -> p (a n)"), IDB[:, :]).then_inc(s_it, 1)

        def pe_unit(pe, g, u):
            if u == 0:
                pe.wait_ge(s_nmx[g.slot], (g.round + 1) * 48)
            wait(pe, s_exp, g.n * UNITS + u - 1)
            for s, blocks, at in unit_parts(u):
                w = blocks * P
                last = nc.tensor.matmul(PS[:, u % 2, at:at + w], KS[0:ROWS, g.slot, s, T - w:T - w + P],
                                        QS[0:ROWS, g.slot, s, T - w:T], start=True, stop=True)
            last.then_inc(s_unit, 1)

        def pe_values(pe, g, j):
            if j == 0:
                pe.wait_ge(s_msk, (g.n + 1) * MASKS)
                pe.wait_ge(s_vs, g.n + 1)
                wait(pe, s_pve, g.n)
            for s in range(GS):
                u, at = exp_place(s, j)
                src = PT[:, g.par, u, at:at + T - j * P]
                last = nc.tensor.matmul(PS[VW * s:VW * (s + 1), 6, j * P:T], VS[:, g.par, j, s // 2, :], src,
                                        start=(j == 0), stop=(j == 2), skip_group_check=True)
            if j == 2:
                last.then_inc(s_pv, 1)

        def pe_transpose_values(pe, g):
            pe.wait_ge(s_pve, g.n + 1)
            pe.wait_ge(s_u1, g.n + 1)
            for tb in range(NT):
                last = nc.tensor.transpose(PS[:, 7, tb * P:(tb + 1) * P], OTS[:, g.par, tb * P:(tb + 1) * P], ID[:, :])
            last.then_inc(s_ot, 1)

        def pe_step(pe, g_max, g_unit, g_val, g_tr):
            for k in range(ITEMS):
                if g_unit.valid() and k < UNITS:
                    pe_unit(pe, g_unit, k)
                if g_max.valid():
                    pe_max_tile(pe, g_max, k)
                if g_val.valid() and k in VALUE_TURNS:
                    pe_values(pe, g_val, (0, 1, 3, 2)[VALUE_TURNS.index(k)])
                if g_tr.valid() and k == 4:
                    pe_transpose_values(pe, g_tr)

        @block.tensor
        def _(pe):
            pe.wait_ge(s_sc, 1)
            for a, which in enumerate((0, 1, 3, 4)):
                for m in range(KC):
                    at = (a * KC + m) * B
                    for k in range(KC):
                        last = nc.tensor.matmul(PS[:, 7, at:at + B], WMOD[:, k, which * E + m * P:which * E + (m + 1) * P],
                                                SC[:, k, :], start=(k == 0), stop=(k == KC - 1))
            last.then_inc(s_modp, 1)
            for b in range(B):
                for k in range(KC):
                    last = nc.tensor.matmul(PS[:, 5 + b, :], SC[:, k, b:b + 1].to_broadcast([P, P]),
                                            WMOD[:, k, :].rearrange("p (a n) -> p a n", a=2)[:, :, 2 * E:3 * E],
                                            start=(k == 0), stop=(k == KC - 1))
                last.then_inc(s_modp, 1)

            def transposes(src, bank, b, k, count):
                for tb in range(NT):
                    last = nc.tensor.transpose(PS[:, bank, tb * P:(tb + 1) * P],
                                               src[:, b * NT + tb, k * P:(k + 1) * P], ID[:, :])
                last.then_inc(count, 1)

            pe.wait_ge(s_misc, 96)
            for n in range(B * KC):
                if n % KC == 0:
                    pe.wait_ge(s_ln, (n // KC + 1) * NT)
                transposes(XN, n, n // KC, n % KC, s_tr)
            pe.wait_ge(s_wqkv, 16)
            pe.wait_ge(s_modv, B)
            for n in range(4 * B):
                b, m, side = n // 4, n // 2 % 2, n % 2
                pe.wait_ge(s_ht, (b + 1) * KC)
                if n >= 2:
                    pe.wait_ge(s_rot, n - 1)
                for i in range(2):
                    for k in range(KC):
                        at = (2 * side + i) * E + m * P
                        last = nc.tensor.matmul(PS[:, 4 + 2 * (n % 2) + i, :], WQKV[:, k, at:at + P], HT[:, b, k, :],
                                                start=(k == 0), stop=(k == KC - 1))
                last.then_inc(s_proj, 1)
            for n in range(B * NT // 2):
                for j in range(2):
                    for k in range(KC):
                        tb = n % 2 * 2 + j
                        last = nc.tensor.matmul(PS[:, n, j * E:(j + 1) * E], HT[:, n // 2, k, tb * P:(tb + 1) * P],
                                                WQKV[:, k, 4 * E:5 * E], start=(k == 0), stop=(k == KC - 1))
                last.then_inc(s_vp, 1)

            pe.wait_ge(s_rot, 4 * B)
            def low_pass_tile(n):
                bank, at = tile_place(n)
                b, tb = n // NT, n % NT
                for k in range(NT):
                    last = nc.tensor.matmul(PS[:, bank, at:at + E], LP[:, k, tb * P:(tb + 1) * P],
                                            U[:, b * GB:(b + 1) * GB, k, :], start=(k == 0), stop=(k == NT - 1))
                last.then_inc(s_lp, 1)

            pe.wait_ge(s_vr, B * NT)
            pe.wait_ge(s_ones, 1)
            none = Group(-1)
            for g in range(2):
                for k in range(ITEMS):
                    pe_max_tile(pe, Group(g), k)
            pe_step(pe, Group(2), Group(0), none, none)
            pe_step(pe, Group(3), Group(1), Group(0), none)
            with pe.Fori(0, 3) as i:
                for u in range(RING):
                    pe_step(pe, Group(u + 4, i), Group(u + 2, i), Group(u + 1, i), Group(u, i))
            last = NG * ITEMS - 1
            pe.wait_ge(s_split, NG)
            pe.wait_ge(s_itf, last - RING + 1)
            pe_transpose_max(pe, (NG - 1) % 2, MAX_BANK + last % RING)
            pe_step(pe, none, Group(14), Group(13), Group(12))
            pe.wait_ge(s_u, GB + 2)
            pe.wait_ge(s_itf, NG * ITEMS)
            pe.wait_ge(s_att, 48)
            low_pass_tile(0)
            pe_step(pe, none, Group(15), Group(14), Group(13))
            low_pass_tile(1)
            low_pass_tile(2)
            pe_step(pe, none, none, Group(15), Group(14))
            low_pass_tile(3)
            pe_transpose_values(pe, Group(15))

            pe.wait_ge(s_u, NG + 2)
            pe.wait_ge(s_exp, NG * UNITS)
            for n in range(NT, B * NT):
                low_pass_tile(n)
            pe.wait_ge(s_u1, NG + 1)
            for b in range(B):
                pe.wait_ge(s_an, (b + 1) * NT)
                for k in range(KC):
                    transposes(AN, 4 + b * KC + k, b, k, s_at)
                pe.wait_ge(s_atc, (b + 1) * KC)
                for tb in range(NT):
                    bank, at = tile_place(b * NT + tb)
                    for k in range(KC):
                        last = nc.tensor.matmul(PS[:, bank, at:at + E], AT[:, b, k, tb * P:(tb + 1) * P],
                                                WOS[:, k, :], start=(k == 0), stop=(k == KC - 1))
                    last.then_inc(s_op, 1)
            for n in range(B * KC):
                if n % KC == 0:
                    pe.wait_ge(s_ln, B * NT + (n // KC + 1) * NT)
                transposes(XN, 4 + n, n // KC, n % KC, s_tr)
            pe.wait_ge(s_ht, 2 * B * KC)
            for n in range(B * NT):
                b, tb = n // NT, n % NT
                for k in range(KC):
                    last = nc.tensor.matmul(PS[:, 6, n * NX:(n + 1) * NX], HT[:, b, k, tb * P:(tb + 1) * P],
                                            WR[:, k, :], start=(k == 0), stop=(k == KC - 1))
            last.then_inc(s_lg, 1)
            pe.wait_ge(s_moe, 48)
            for n, (b, c) in enumerate(BLOCKS):
                if n == AHEAD:
                    pe.wait_ge(s_cwp, 1)
                    for i in range(B):
                        for tb in range(NT):
                            last = nc.tensor.transpose(PS[0:PARTS * NX, 6 + i, tb * P // 2:(tb + 1) * P // 2].bitcast(BF16),
                                                       CWP[:, i * NT + tb].rearrange("p a e -> p (a e)"), IDB[:, :])
                        last.then_inc(s_cwt, 1)
                if (b, c) == (0, 0):
                    pe.wait_ge(s_cwc, B)
                if n >= 2:
                    pe.wait_ge(s_guf, n - 1)
                for i, W in enumerate((WG, WU)):
                    for k in range(KC):
                        last = nc.tensor.matmul(PS[:, n % 2 * 3 + i, :], W[:, k, c * P:(c + 1) * P], HT[:, b, k, :],
                                                start=(k == 0), stop=(k == KC - 1))
                if c < ROUTED:
                    last = nc.tensor.matmul(PS[:, n % 2 * 3 + 2, :], PICK[:, c * P:(c + 1) * P], CWT[:, b, :],
                                            start=True, stop=True)
                last.then_inc(s_gu, 1)
            for b in range(B):
                pe.wait_ge(s_guf, B * NF)
                for tb in range(NT):
                    for c in range(NF):
                        last = nc.tensor.matmul(PS[:, b * 2 + tb // 2, tb % 2 * E:(tb % 2 + 1) * E],
                                                FEAT[b][:, c, tb * P:(tb + 1) * P], WD[:, c, :],
                                                start=(c == 0), stop=(c == NF - 1))
                    last.then_inc(s_dn, 1)


def constants():
    pos = np.arange(T, dtype=np.float64)
    inv = 1.0 / 10000.0 ** (np.arange(0, D, 2, dtype=np.float32) / np.float32(D))
    ang = np.outer(np.arange(T, dtype=np.float32), inv.astype(np.float32)).astype(np.float64)
    d = np.arange(P) // H
    cos = np.cos(ang[:, d // 2]).T
    sin = np.sin(ang[:, d // 2]).T * np.where(d % 2, 1.0, -1.0)[:, None]
    scale = float(D) ** -0.5
    rope = np.stack([cos * scale, sin * scale, cos, sin], axis=1).astype(np.float32)
    freq = np.linspace(0.0, 1.0, T // 2 + 1)
    filt = np.exp(-0.5 * (freq / 0.15) ** 2)
    wave = np.fft.irfft(filt, n=T)
    low_pass = wave[(np.arange(T)[:, None] - np.arange(T)[None, :]) % T].astype(np.float32)
    causal = np.zeros((P, T), np.float32)
    causal[:, T - P:] = np.where(np.arange(P)[None, :] > np.arange(P)[:, None], -1e30, 0.0)
    ident = np.eye(P, dtype=np.float32)
    picks = np.zeros((PARTS, NX, ROUTED * P), np.float32)
    picks[:, np.arange(ROUTED * P) // F, np.arange(ROUTED * P)] = 0.5
    return rope, low_pass, causal, ident, picks.reshape(PARTS * NX, ROUTED * P)


def kernel(**inputs):
    import ml_dtypes
    import concourse.bacc as bacc
    from concourse.bass_utils import run_bass_kernel_spmd

    a = {k.replace("L0_", ""): np.asarray(v) for k, v in inputs.items()}
    rope, low_pass, causal, ident, picks = constants()
    d, s = np.arange(D), np.arange(H)
    order = np.concatenate([(m * H + s[None, :]) * D + d[:, None] for m in range(KC)]).reshape(-1)
    twin = np.concatenate([(m * H + s[None, :]) * D + (d ^ 1)[:, None] for m in range(KC)]).reshape(-1)
    wq, wk = a["attn_Wq"], a["attn_Wk"]

    def experts(w, sw):
        w = np.concatenate([np.transpose(w, (2, 0, 1)).reshape(E, NX * F), sw.T], axis=1)
        return np.pad(w, ((0, 0), (0, NF * P - w.shape[1])))

    down = np.concatenate([np.transpose(a["ffn_w_down"], (0, 2, 1)).reshape(NX * F, E), a["ffn_sw_down"].T])
    lam = np.concatenate([a["attn_lambda_" + k] for k in ("q1", "k1", "q2", "k2")])
    arrays = {
        "x": a["attn_query"], "c_t": a["c"].T, "w_mod": a["wmod"],
        "w_qkv": np.concatenate([wq[:, order], wq[:, twin], wk[:, order], wk[:, twin], a["attn_Wv"]], axis=1),
        "w_out": a["attn_Wout"], "rms_w": np.tile(a["attn_rms_weight"], H), "lam": np.tile(lam[None, :], (P, 1)),
        "w_router": a["ffn_gate_weight"].T,
        "w_gate": experts(a["ffn_w_gate"], a["ffn_sw_gate"]), "w_up": experts(a["ffn_w_up"], a["ffn_sw_up"]),
        "w_down": np.pad(down, ((0, NF * P - down.shape[0]), (0, 0))),
        "rope": rope, "low_pass": low_pass, "causal": causal, "ident": ident,
        "ident_b": ident.astype(ml_dtypes.bfloat16), "picks": picks.astype(ml_dtypes.bfloat16),
    }
    for name in ("c_t", "w_mod", "w_qkv", "w_out", "w_router", "w_gate", "w_up", "w_down", "low_pass"):
        v = arrays[name]
        arrays[name] = v.reshape(-1, P, v.shape[1]).transpose(1, 0, 2)
    arrays["rms_w"] = arrays["rms_w"].reshape(KC, P).T
    nc = bacc.Bacc("TRN2", target_bir_lowering=False, num_devices=1)
    feed, args = {}, []
    for name, v in arrays.items():
        v = np.ascontiguousarray(v)
        feed["in_" + name] = v
        args.append(nc.dram_tensor("in_" + name, v.shape, mybir.dt.from_np(v.dtype), kind="ExternalInput").ap())
    args.append(nc.dram_tensor("out", (B, T, E), F32, kind="ExternalOutput").ap())
    attention_block(nc, *args)
    r = run_bass_kernel_spmd(nc, [feed], core_ids=[0])
    return r.results[0]["out"]
```
